# Optimizing a Trainium2 kernel written in Bass

```python
import numpy as np
import jax
import jax.numpy as jnp

def _softmax(x, axis=-1):
    return jax.nn.softmax(x, axis=axis)

def _gelu(x):
    return jax.nn.gelu(x, approximate=True)

def _silu(x):
    return jax.nn.silu(x)

def _sigmoid(x):
    return jax.nn.sigmoid(x)

def _layernorm(x, axis=-1, eps=1e-05):
    m = jnp.mean(x, axis=axis, keepdims=True)
    v = jnp.var(x, axis=axis, keepdims=True)
    return (x - m) / jnp.sqrt(v + eps)

def _scatter_add(tgt, idx, src, axis=0):
    return tgt.at[idx].add(src)

def _segment_sum(src, seg, n):
    return jax.ops.segment_sum(src, seg, n)
kernel_name = 'mk_hybrid_d1_jaxref_r8_0af0e0'

def setup_inputs(seed: int=0):
    np.random.seed(seed)
    _w = jnp.asarray

    def _L0_attn_a_setup():
        import jax, jax.numpy as jnp
        import numpy as np
        key = jax.random.key(seed)
        ks = jax.random.split(key, 8)
        B, L, DIM, INNER = (4, 512, 128, 64)
        return {'x': jax.random.normal(ks[0], (B, L, DIM), dtype=jnp.float32), 'w_a': jax.random.normal(ks[1], (2 * INNER, DIM), dtype=jnp.float32) * DIM ** (-0.5), 'w_x': jax.random.normal(ks[2], (2 * INNER, DIM), dtype=jnp.float32) * DIM ** (-0.5), 'w_out': jax.random.normal(ks[3], (DIM, INNER), dtype=jnp.float32) * INNER ** (-0.5), 'mat_v_real': jax.random.normal(ks[4], (INNER, INNER), dtype=jnp.float32), 'mat_v_imag': jax.random.normal(ks[5], (INNER, INNER), dtype=jnp.float32), 'last_hidden_real': jax.random.normal(ks[6], (INNER,), dtype=jnp.float32), 'last_hidden_imag': jax.random.normal(ks[7], (INNER,), dtype=jnp.float32)}
    _L0_attn_a_in = _L0_attn_a_setup()

    def _L0_attn_b_setup():
        import jax, jax.numpy as jnp
        import numpy as np
        B, L, E, H = (2, 512, 128, 16)
        D = E // H
        CHUNK = 32

        def _linear_attention(x, W_qkv, W_out):
            Bz, Lz, Ez = x.shape
            scale = D ** (-0.5)
            qkv = x @ W_qkv.T
            qkv = qkv.reshape(Bz, Lz, 3, H, D).transpose(2, 0, 3, 1, 4)
            q, k, v = (qkv[0], qkv[1], qkv[2])
            q = (jax.nn.elu(q) + 1.0) * scale
            k = jax.nn.elu(k) + 1.0
            nc = Lz // CHUNK

            def to_chunks(t):
                return t.reshape(Bz, H, nc, CHUNK, D).transpose(2, 0, 1, 3, 4)
            qc, kc, vc = (to_chunks(q), to_chunks(k), to_chunks(v))
            causal = jnp.tril(jnp.ones((CHUNK, CHUNK), dtype=x.dtype))

            def step(carry, inp):
                S, Z = carry
                qi, ki, vi = inp
                attn = jnp.einsum('bhld,bhmd->bhlm', qi, ki) * causal
                num = jnp.einsum('bhlm,bhme->bhle', attn, vi) + jnp.einsum('bhld,bhde->bhle', qi, S)
                den = attn.sum(-1) + jnp.einsum('bhld,bhd->bhl', qi, Z)
                S = S + jnp.einsum('bhmd,bhme->bhde', ki, vi)
                Z = Z + ki.sum(axis=2)
                return ((S, Z), (num, den))
            S0 = jnp.zeros((Bz, H, D, D), dtype=x.dtype)
            Z0 = jnp.zeros((Bz, H, D), dtype=x.dtype)
            _, (num, den) = jax.lax.scan(step, (S0, Z0), (qc, kc, vc))
            num = num.transpose(1, 2, 0, 3, 4).reshape(Bz, H, Lz, D)
            den = den.transpose(1, 2, 0, 3).reshape(Bz, H, Lz)
            den = jnp.maximum(den, 1e-06)
            out = num / den[..., None]
            out = out.transpose(0, 2, 1, 3).reshape(Bz, Lz, Ez)
            return out @ W_out.T
        key = jax.random.key(seed)
        k1, k2, k3 = jax.random.split(key, 3)
        x = jax.random.normal(k1, (B, L, E), dtype=jnp.float32)
        W_qkv = jax.random.normal(k2, (3 * E, E), dtype=jnp.float32) * 0.02
        W_out = jax.random.normal(k3, (E, E), dtype=jnp.float32) * 0.02
        return {'x': x, 'W_qkv': W_qkv, 'W_out': W_out}
    _L0_attn_b_in = _L0_attn_b_setup()

    def _L0_ffn_setup():
        import jax, jax.numpy as jnp
        import numpy as np
        import math
        B, L, D = (4, 512, 128)
        F = 512
        E = 16
        CAP_FACTOR = 1.0
        EPS = 1e-05
        key = jax.random.key(seed)
        ks = jax.random.split(key, 8)
        std = 0.02
        return {'x': jax.random.normal(ks[0], (B, L, D), dtype=jnp.float32), 'norm_weight': jnp.ones((D,), dtype=jnp.float32), 'router_weight': jax.random.normal(ks[1], (E, D), dtype=jnp.float32) * std, 'router_bias': jnp.zeros((E,), dtype=jnp.float32), 'fc1_weight': jax.random.normal(ks[2], (E, F, D), dtype=jnp.float32) * std, 'fc1_bias': jnp.zeros((E, F), dtype=jnp.float32), 'fc2_weight': jax.random.normal(ks[3], (E, D, F), dtype=jnp.float32) * std, 'fc2_bias': jnp.zeros((E, D), dtype=jnp.float32)}
    _L0_ffn_in = _L0_ffn_setup()
    _d = {'L0_attn_a_x': _L0_attn_a_in['x'], 'L0_attn_a_w_a': _L0_attn_a_in['w_a'], 'L0_attn_a_w_x': _L0_attn_a_in['w_x'], 'L0_attn_a_w_out': _L0_attn_a_in['w_out'], 'L0_attn_a_mat_v_real': _L0_attn_a_in['mat_v_real'], 'L0_attn_a_mat_v_imag': _L0_attn_a_in['mat_v_imag'], 'L0_attn_a_last_hidden_real': _L0_attn_a_in['last_hidden_real'], 'L0_attn_a_last_hidden_imag': _L0_attn_a_in['last_hidden_imag'], 'L0_attn_b_W_qkv': _L0_attn_b_in['W_qkv'], 'L0_attn_b_W_out': _L0_attn_b_in['W_out'], 'L0_ffn_norm_weight': _L0_ffn_in['norm_weight'], 'L0_ffn_router_weight': _L0_ffn_in['router_weight'], 'L0_ffn_router_bias': _L0_ffn_in['router_bias'], 'L0_ffn_fc1_weight': _L0_ffn_in['fc1_weight'], 'L0_ffn_fc1_bias': _L0_ffn_in['fc1_bias'], 'L0_ffn_fc2_weight': _L0_ffn_in['fc2_weight'], 'L0_ffn_fc2_bias': _L0_ffn_in['fc2_bias']}
    _x0 = _d['L0_attn_a_x']
    _d['L0_attn_a_x'] = jax.random.normal(jax.random.fold_in(jax.random.key(seed), 1), (2, 2048, 128), dtype=_x0.dtype)
    del _x0
    return _d

def reference(L0_attn_a_x, L0_attn_a_w_a, L0_attn_a_w_x, L0_attn_a_w_out, L0_attn_a_mat_v_real, L0_attn_a_mat_v_imag, L0_attn_a_last_hidden_real, L0_attn_a_last_hidden_imag, L0_attn_b_W_qkv, L0_attn_b_W_out, L0_ffn_norm_weight, L0_ffn_router_weight, L0_ffn_router_bias, L0_ffn_fc1_weight, L0_ffn_fc1_bias, L0_ffn_fc2_weight, L0_ffn_fc2_bias):

    def _L0_attn_a_ref(x, w_a, w_x, w_out, mat_v_real, mat_v_imag, last_hidden_real, last_hidden_imag):
        import jax, jax.numpy as jnp
        import numpy as np
        b, l, dim = x.shape
        inner = mat_v_real.shape[0]
        V = jax.lax.complex(mat_v_real, mat_v_imag)
        Vinv = jnp.linalg.inv(V)
        h0 = jax.lax.complex(last_hidden_real, last_hidden_imag)
        xf = x.astype(jnp.float32)
        a2 = (xf @ w_a.T).reshape(b, l, inner, 2)
        a_mag2 = a2[..., 0] ** 2 + a2[..., 1] ** 2
        a = jax.lax.complex(a2[..., 0], a2[..., 1]) * (jax.lax.rsqrt(a_mag2) * jax.nn.sigmoid(jnp.log(a_mag2)))
        x2 = (xf @ w_x.T).reshape(b, l, inner, 2)
        x_mag2 = x2[..., 0] ** 2 + x2[..., 1] ** 2
        xc = jax.lax.complex(x2[..., 0], x2[..., 1]) * (jax.lax.rsqrt(x_mag2) * x_mag2)
        x_roll = jnp.concatenate([jnp.broadcast_to(h0, (b, 1, inner)), xc[:, :-1]], axis=1)
        u = jnp.einsum('mn,bln->blm', Vinv, x_roll)

        def combine(c1, c2):
            a1, b1 = c1
            a2_, b2 = c2
            return (a2_ * a1, a2_ * b1 + b2)
        _, s = jax.lax.associative_scan(combine, (a, a * u), axis=1)
        h = jnp.einsum('mn,bln->blm', V, s) + xc
        return (h.real @ w_out.T).astype(x.dtype)

    def _L0_attn_b_ref(x, W_qkv, W_out):
        import jax, jax.numpy as jnp
        import numpy as np
        B, L, E, H = (2, 512, 128, 16)
        D = E // H
        CHUNK = 32

        def _linear_attention(x, W_qkv, W_out):
            Bz, Lz, Ez = x.shape
            scale = D ** (-0.5)
            qkv = x @ W_qkv.T
            qkv = qkv.reshape(Bz, Lz, 3, H, D).transpose(2, 0, 3, 1, 4)
            q, k, v = (qkv[0], qkv[1], qkv[2])
            q = (jax.nn.elu(q) + 1.0) * scale
            k = jax.nn.elu(k) + 1.0
            nc = Lz // CHUNK

            def to_chunks(t):
                return t.reshape(Bz, H, nc, CHUNK, D).transpose(2, 0, 1, 3, 4)
            qc, kc, vc = (to_chunks(q), to_chunks(k), to_chunks(v))
            causal = jnp.tril(jnp.ones((CHUNK, CHUNK), dtype=x.dtype))

            def step(carry, inp):
                S, Z = carry
                qi, ki, vi = inp
                attn = jnp.einsum('bhld,bhmd->bhlm', qi, ki) * causal
                num = jnp.einsum('bhlm,bhme->bhle', attn, vi) + jnp.einsum('bhld,bhde->bhle', qi, S)
                den = attn.sum(-1) + jnp.einsum('bhld,bhd->bhl', qi, Z)
                S = S + jnp.einsum('bhmd,bhme->bhde', ki, vi)
                Z = Z + ki.sum(axis=2)
                return ((S, Z), (num, den))
            S0 = jnp.zeros((Bz, H, D, D), dtype=x.dtype)
            Z0 = jnp.zeros((Bz, H, D), dtype=x.dtype)
            _, (num, den) = jax.lax.scan(step, (S0, Z0), (qc, kc, vc))
            num = num.transpose(1, 2, 0, 3, 4).reshape(Bz, H, Lz, D)
            den = den.transpose(1, 2, 0, 3).reshape(Bz, H, Lz)
            den = jnp.maximum(den, 1e-06)
            out = num / den[..., None]
            out = out.transpose(0, 2, 1, 3).reshape(Bz, Lz, Ez)
            return out @ W_out.T
        return _linear_attention(x, W_qkv, W_out)

    def _L0_ffn_ref(x, norm_weight, router_weight, router_bias, fc1_weight, fc1_bias, fc2_weight, fc2_bias):
        import jax, jax.numpy as jnp
        import numpy as np
        import math
        B, L, D = (4, 512, 128)
        F = 512
        E = 16
        CAP_FACTOR = 1.0
        EPS = 1e-05
        b, l, d = x.shape
        n_tokens = b * l
        n_experts = router_weight.shape[0]
        capacity = max(1, math.ceil(CAP_FACTOR * n_tokens / n_experts))
        top_k = min(capacity, n_tokens)
        xf = x.reshape(n_tokens, d)
        rms = jnp.sqrt(jnp.mean(xf * xf, axis=-1, keepdims=True) + EPS)
        xn = xf / rms * norm_weight
        logits = xn @ router_weight.T + router_bias
        probs = jax.nn.softmax(logits, axis=-1)
        _, idx = jax.lax.top_k(logits.T, top_k)
        xe = xn[idx]
        h = jnp.einsum('ecd,efd->ecf', xe, fc1_weight) + fc1_bias[:, None, :]
        h = jax.nn.gelu(h, approximate=False)
        y = jnp.einsum('ecf,edf->ecd', h, fc2_weight) + fc2_bias[:, None, :]
        gates = jnp.take_along_axis(probs.T, idx, axis=1)
        flat_idx = idx.reshape(-1)
        contrib = (y * gates[:, :, None]).reshape(-1, d)
        output = jnp.zeros((n_tokens, d), dtype=x.dtype).at[flat_idx].add(contrib)
        gate_sums = jnp.zeros((n_tokens, 1), dtype=x.dtype).at[flat_idx].add(gates.reshape(-1, 1))
        assigned = gate_sums > 0
        output = jnp.where(assigned, output / jnp.where(assigned, gate_sums, 1.0), output)
        return output.reshape(b, l, d)
    x = L0_attn_a_x
    x = x + _L0_attn_a_ref(_layernorm(x, axis=-1), L0_attn_a_w_a, L0_attn_a_w_x, L0_attn_a_w_out, L0_attn_a_mat_v_real, L0_attn_a_mat_v_imag, L0_attn_a_last_hidden_real, L0_attn_a_last_hidden_imag)
    x = x + _L0_ffn_ref(_layernorm(x, axis=-1), L0_ffn_norm_weight, L0_ffn_router_weight, L0_ffn_router_bias, L0_ffn_fc1_weight, L0_ffn_fc1_bias, L0_ffn_fc2_weight, L0_ffn_fc2_bias)
    x = x + _L0_attn_b_ref(_layernorm(x, axis=-1), L0_attn_b_W_qkv, L0_attn_b_W_out)
    x = x + _L0_ffn_ref(_layernorm(x, axis=-1), L0_ffn_norm_weight, L0_ffn_router_weight, L0_ffn_router_bias, L0_ffn_fc1_weight, L0_ffn_fc1_bias, L0_ffn_fc2_weight, L0_ffn_fc2_bias)
    return x

_drawn_inputs = setup_inputs


def setup_inputs(seed=0):
    import zlib

    import numpy as np

    out = dict(_drawn_inputs(seed))
    spreads = {'L0_ffn_norm_weight': (1.0, 0.6),
     'L0_ffn_router_bias': (0.0, 0.8),
     'L0_ffn_fc1_bias': (0.0, 0.8),
     'L0_ffn_fc2_bias': (0.0, 0.8)}
    factors = {'L0_attn_a_last_hidden_real': 8.0,
     'L0_attn_a_last_hidden_imag': 8.0,
     'L0_attn_b_W_qkv': 8.0,
     'L0_attn_b_W_out': 8.0,
     'L0_ffn_router_weight': 5.319,
     'L0_ffn_fc1_weight': 8.0,
     'L0_ffn_fc2_weight': 8.0}
    for name, (base, spread) in spreads.items():
        noise = np.random.default_rng([zlib.crc32(name.encode()), seed]).standard_normal(out[name].shape)
        drawn = base * np.exp(spread * noise) if base else spread * noise
        out[name] = jnp.asarray(drawn.astype(out[name].dtype))
    for name, factor in factors.items():
        out[name] = (out[name] * factor).astype(out[name].dtype)
    return out
```

```python
from contextlib import ExitStack

import concourse.bass as bass
from concourse import mybir

F32 = mybir.dt.float32
BF16 = mybir.dt.bfloat16
F16 = mybir.dt.float16
I32 = mybir.dt.int32
U32 = mybir.dt.uint32
ALU = mybir.AluOpType
ACT = mybir.ActivationFunctionType
AX = mybir.AxisListType

P = 128
EPS = 1e-5


class Count:

    def __init__(self, engine, sem):
        self.engine, self.sem, self.n = engine, sem, 0

    def did(self, instruction):
        instruction.then_inc(self.sem, 1)
        self.n += 1

    def settle(self):
        self.engine.wait_ge(self.sem, self.n)

    def step(self, instruction):
        self.did(instruction)
        self.settle()


def build(nc, x, wa, wx, wo, vr, vi, vrT, viT, h0r, h0i, wqkvT, woutT, nw, rwT, rb, f1T, f1b, f2T, f2b, out):
    NB, LT, D = x.shape
    INNER = vr.shape[0]
    NTOK = NB * LT
    NT = NTOK // P
    TPG = 4
    NG = NT // TPG
    GW = TPG * P
    NK = LT // GW
    LEVELS = LT.bit_length() - 1
    NE = rwT.shape[1]
    NF = f1T.shape[2]
    FT = NF // P
    CAP = NTOK // NE
    TW = D + NE
    AW = D + 1
    NCH = P // NE

    tab = [nc.dram_tensor(f"tab{f}", [NTOK, TW], F32).ap() for f in range(2)]
    acc = [[nc.dram_tensor(f"acc{f}{i}", [NTOK, AW], F32).ap() for i in range(2)] for f in range(2)]
    cntd = [nc.dram_tensor(f"cntd{f}", [P, GW], F32).ap() for f in range(2)]

    with ExitStack() as ctx:
        def sb(name, shape, dt=F32):
            return ctx.enter_context(nc.sbuf_tensor(name, shape, dt))

        def sem(name):
            return ctx.enter_context(nc.semaphore(name))

        ps = ctx.enter_context(nc.psum_tensor("ps", [P, 8, GW], F32))
        xs = sb("xs", [P, NT, D])
        xT = sb("xT", [P, NTOK])
        tb = sb("tb", [P, NT, TW])
        tbf = tb[:, :, :].rearrange("p a b -> p (a b)")
        ident = sb("ident", [P, P])
        ones = sb("ones", [P, P])
        bst = sb("bst", [P, NT, 6])
        sd = sb("sd", [P, 8, NT])
        s_mean, s_w, s_vp, s_rt, s_r, s_q, s_d = (sd[:, i, :] for i in range(7))
        stage = sb("stage", [P, 2 * TPG, D])
        waT = sb("waT", [P, 4, INNER])
        VV = sb("VV", [INNER, 4, INNER])
        RT = sb("RT", [P, P])
        Rm = sb("Rm", [P, P])
        XX = sb("XX", [P, 2, P])
        Zm = sb("Zm", [P, P])
        aI = sb("aI", [P, 2, P])
        BD = sb("BD", [P, 3, P])
        nrm = sb("nrm", [P, 4])
        arena = sb("arena", [P, 18440])
        off = [0]

        def carve(n):
            off[0] += n
            return arena[:, off[0] - n:off[0]]
        av = carve(2 * LT).rearrange("p (c t) -> p c t", c=2)
        lev = carve(2 * LT).rearrange("p (c t) -> p c t", c=2)
        SS = carve(2 * LT).rearrange("p (c t) -> p c t", c=2)
        XC = carve(2 * (LT + 1)).rearrange("p (c t) -> p c t", c=2)
        sq = carve(4 * GW).rearrange("p (c t) -> p c t", c=4)
        assert off[0] <= 18440
        mag = tbf[:, 0:2 * GW].rearrange("p (c t) -> p c t", c=2)
        rt2 = tbf[:, 2 * GW:4 * GW].rearrange("p (c t) -> p c t", c=2)
        rec = tbf[:, 4 * GW:5 * GW]
        MB = tbf[:, 3600:3600 + 3 * 2 * D].rearrange("p (i b d) -> p i b d", i=3, b=NB)
        T1 = sq[:, 0:2, :]
        T2 = sq[:, 2:4, :]

        f1w = sb("f1w", [P, NE, NF])
        f2w = sb("f2w", [P, NE, FT, D])
        b1 = sb("b1", [P, NE, FT])
        nwc = sb("nwc", [P, 1])
        rwp = sb("rwp", [P, 2, 32])
        rbc = sb("rbc", [P, 1])
        same = sb("same", [P, P], F16)
        before = sb("before", [P, P], F16)
        differ = sb("differ", [P, P], F16)
        srow = sb("srow", [P, CAP], F16)
        scol = sb("scol", [P, 2])
        bits = sb("bits", [P, 48], U32)
        nb = sb("nb", [P, 48], U32)
        ione = sb("ione", [P, 32], U32)
        ish = sb("ish", [P, 32], U32)
        tk = sb("tk", [P, 16])
        tku = tk[:, :].bitcast(U32)
        cn = sb("cn", [P, 4], F16)
        idx = sb("idx", [P, 2 * NE], U32)
        zero = tbf[:, 3000:3000 + TPG * AW]
        off[0] = 0
        L = carve(GW)
        cnt = carve(GW)
        csg = carve(GW)
        exs = carve(GW)
        lesum = carve(2 * NE)
        rinv = carve(NT)
        smx = carve(NT)
        gt, eq = (carve(GW // 2).bitcast(F16) for _ in range(2))
        cs16, cd16 = (carve(GW // 2).bitcast(F16) for _ in range(2))
        acc1 = arena[:, off[0]:off[0] + NT * AW].rearrange("p (t w) -> p t w", w=AW)
        G16 = carve(NE * CAP // 2).bitcast(F16).rearrange("p (e s) -> p e s", e=NE)
        RX = 4
        XE = carve(RX * 2 * TW).rearrange("p (r h w) -> p r h w", r=RX, h=2)
        xeT = carve(2 * CAP).rearrange("p (r s) -> p r s", r=2)
        hT = carve(2 * FT * CAP).rearrange("p (r f s) -> p r f s", r=2, f=FT)
        yv = carve(2 * 2 * AW).rearrange("p (r h w) -> p r h w", r=2, h=2)
        b2 = carve(NE * D).rearrange("p (e d) -> p e d", e=NE)
        assert off[0] <= 18440

        HD = 8
        wqkv = sb("wqkv", [P, 3, P])
        wou = sb("wou", [P, D])
        B8 = sb("B8", [P, P])
        causal = sb("causal", [P, P])
        rowm = sb("rowm", [P, 4])
        zc = sb("zc", [P, 1])
        off[0] = 0
        qn, kT, kt, vn, rden, On = (carve(2 * GW).rearrange("p (r t) -> p r t", r=2) for _ in range(6))
        vpad = carve(2 * TPG * 512).rearrange("p (r t n) -> p r t n", r=2, t=TPG)
        att = carve(2 * 2048).rearrange("p (r o n) -> p r o n", r=2, o=4)
        exq, exk, Zc, exz = carve(GW), carve(GW), carve(GW), carve(GW)
        S = carve(2 * P).rearrange("p (r n) -> p r n", r=2)
        Stmp = carve(P)
        assert off[0] <= 18440
        Q4 = tbf[:, 0:2 * 4 * GW].rearrange("p (r i t) -> p r i t", r=2, i=4)
        wb_in = sem("wb_in")
        vpad_zero = sem("vpad_zero")
        b8_ready = sem("b8_ready")
        q_prod, q_min, q_exp, q_ready, q4_ready = (sem(n) for n in ("q_prod", "q_min", "q_exp", "q_ready", "q4_ready"))
        k_prod, k_min, k_exp, k_ready = (sem(n) for n in ("k_prod", "k_min", "k_exp", "k_ready"))
        v_prod, v_ready, kt_prod, kt_ready = (sem(n) for n in ("v_prod", "v_ready", "kt_prod", "kt_ready"))
        qz_ready, den_prod, den_ready = (sem(n) for n in ("qz_ready", "den_prod", "den_ready"))
        sc_prod, sc_masked, num_prod, num_used, s_upd = (sem(n) for n in ("sc_prod", "sc_masked", "num_prod", "num_used", "s_upd"))
        fin_prod, x3_ready = sem("fin_prod"), sem("x3_ready")

        wf_in = [sem(f"wf_in{q}") for q in range(4)]
        router_in, b2_in, fb_in = sem("router_in"), sem("b2_in"), sem("fb_in")
        zeroed, tab_stored, cnt_stored, seg_in = sem("zeroed"), sem("tab_stored"), sem("cnt_stored"), sem("seg_in")
        xe_in = [sem(f"xe_in{r}") for r in range(RX)]
        scattered = [sem(f"scattered{i}") for i in range(2)]
        acc_in = [sem(f"acc_in{g}") for g in range(NG)]
        logit_prod, logit_T, logit_ready, exp_in, exped, tab_ready = (sem(n) for n in ("logit_prod", "logit_T", "logit_ready", "exp_in", "exped", "tab_ready"))
        counted, totalled = sem("counted"), sem("totalled")
        cand_ready, cnt_ready, seg16, seg_diff, onehot, slots_ready, idx_ready = (
            sem(n) for n in ("cand_ready", "cnt_ready", "seg16", "seg_diff", "onehot", "slots_ready", "idx_ready"))
        xe_T, xeT_ready, h_prod, h_ready, y_prod, y_ready, x_ready = (
            sem(n) for n in ("xe_T", "xeT_ready", "h_prod", "h_ready", "y_prod", "y_ready", "x_ready"))
        NR = 32
        BITS = 10
        NCOUNT = NR + 2

        x_in = [sem(f"x_in{g}") for g in range(NG)]
        wab_in, inv_in, wo_in, h0_in = sem("wab_in"), sem("inv_in"), sem("wo_in"), sem("h0_in")
        w_in = sem("w_in")
        stored = sem("stored")
        consts = sem("consts")
        dstep, pstep, gstep = sem("dstep"), sem("pstep"), sem("gstep")
        vp_ready, root_ready = sem("vp_ready"), sem("root_ready")
        normed, transposed, xT_ready = sem("normed"), sem("transposed"), sem("xT_ready")
        nw_sq, nw_norm, nw_Y, nw_Z, nw_X, nw_new = (sem(s) for s in ("nw_sq", "nw_norm", "nw_Y", "nw_Z", "nw_X", "nw_new"))
        bd_ready, mt_prod, mt_ready = sem("bd_ready"), sem("mt_prod"), sem("mt_ready")
        projected, squared, mag_ready, rooted, proj_used = (sem(s) for s in ("projected", "squared", "mag_ready", "rooted", "proj_used"))
        u_ready, u_used, s_ready = sem("u_ready"), sem("u_used"), sem("s_ready")
        lev_ready, raw_ready = sem("lev_ready"), sem("raw_ready")
        ao_ready, x1_ready = sem("ao_ready"), sem("x1_ready")

        N_WIDE, N_LAST = 18, 6
        HALVES = 2 * (N_WIDE + N_LAST)
        AT_NORM, AT_STEP, AT_COEF = 12, 6, 18
        WA, WB = 3.5, 3.5 * 3.5 / 4

        block = ctx.enter_context(nc.Block())

        @block.sync
        def _(sp):
            for t, src in ((RT[0:64, 0:64], vrT), (RT[64:128, 64:128], vrT), (RT[0:64, 64:128], viT), (RT[64:128, 0:64], viT),
                           (Rm[0:64, 0:64], vr), (Rm[64:128, 64:128], vr), (Rm[0:64, 64:128], vi), (Rm[64:128, 0:64], vi)):
                sp.dma_start(t, src).then_inc(inv_in, 16)
            for g in [b * NK + k for k in range(NK) for b in range(NB)]:
                b, k = divmod(g, NK)
                sp.dma_start(xs[:, g * TPG:(g + 1) * TPG, :],
                             x[b, k * GW:(k + 1) * GW, :].rearrange("(t p) d -> p t d", p=P)).then_inc(x_in[g], 16)
            sp.dma_start(waT[:, 0:2, :], wa).then_inc(wab_in, 16)
            sp.dma_start(waT[:, 2:4, :], wx).then_inc(wab_in, 16)
            for b in range(NB):
                sp.dma_start(XC[64 * b:64 * b + 64, 0, 0:1], h0r).then_inc(h0_in, 16)
                sp.dma_start(XC[64 * b:64 * b + 64, 1, 0:1], h0i).then_inc(h0_in, 16)
            for i in range(4):
                sp.dma_start(VV[:, i, :], vr if i < 2 else vi).then_inc(wo_in, 16)
            sp.wait_ge(consts, 2)
            for b in range(NB):
                sp.dma_start(MB[64 * b:64 * b + 64, 2, b, :], wo).then_inc(wo_in, 16)
            sp.dma_start(nwc[:, :], nw).then_inc(fb_in, 16)
            sp.dma_start(b1[:, :, :], f1b).then_inc(fb_in, 16)
            for c in range(NCH):
                sp.dma_start(rbc[c * NE:(c + 1) * NE, :], rb).then_inc(fb_in, 16)
            sp.dma_start(wqkv[:, :, :], wqkvT.rearrange("d (i n) -> d i n", i=3)).then_inc(wb_in, 16)
            sp.dma_start(wou[:, :], woutT).then_inc(wb_in, 16)
            sp.wait_ge(consts, 2)
            for i in range(2):
                sp.dma_start(rwp[:, i, i * NE:(i + 1) * NE], rwT).then_inc(router_in, 16)
            for q in range(4):
                e = slice(4 * q, 4 * q + 4)
                sp.dma_start(f1w[:, e, :], f1T[:, e, :]).then_inc(wf_in[q], 16)
                sp.dma_start(f2w[:, e, :, :], f2T[:, e, :, :]).then_inc(wf_in[q], 16)
            for f in range(2):
                for g in range(NG):
                    for i in range(2):
                        sp.dma_start(acc[f][i][g * GW:(g + 1) * GW, :].rearrange("(p r) w -> p (r w)", r=TPG), zero
                                     ).then_inc(zeroed, 16)

            def feed(f):
                sp.wait_ge(x1_ready if f == 0 else x3_ready, NG)
                sp.dma_start(b2[:, :, :], f2b.partition_broadcast(P)).then_inc(b2_in, 16)
                sp.wait_ge(tab_ready, f + 1)
                for q in range(4):
                    t = slice(8 * q, 8 * q + 8)
                    sp.dma_start(tab[f][q * 1024:(q + 1) * 1024, :].rearrange("(t p) w -> p t w", p=P), tb[:, t, :]
                                 ).then_inc(tab_stored, 16)
                sp.wait_ge(cnt_ready, f + 1)
                sp.dma_start(cntd[f][:, :], cnt).then_inc(cnt_stored, 16)
                sp.wait_ge(cnt_stored, 16 * (f + 1))
                for c in range(NCH):
                    sp.dma_start(csg[c * NE:(c + 1) * NE, :].rearrange("q (e t) -> q e t", e=NE),
                                 cntd[f][c * NE:(c + 1) * NE, :].rearrange("e (q t) -> q e t", q=NE)).then_inc(seg_in, 16)
                for i in range(2):
                    sp.wait_ge(scattered[i], 32 * NE // 2 * (f + 1))
                for g in range(NG):
                    for i, to in enumerate((tb[:, g * TPG:(g + 1) * TPG, 0:AW], acc1[:, g * TPG:(g + 1) * TPG, :])):
                        sp.dma_start(to, acc[f][i][g * GW:(g + 1) * GW, :].rearrange("(t p) w -> p t w", p=P)
                                     ).then_inc(acc_in[g], 16)

            feed(0)
            feed(1)
            for g in range(NG):
                b, k = divmod(g, NK)
                sp.wait_ge(x_ready, NG + g + 1)
                sp.dma_start(out[b, k * GW:(k + 1) * GW, :].rearrange("(t p) d -> p t d", p=P),
                             xs[:, g * TPG:(g + 1) * TPG, :]).then_inc(stored, 16)
            sp.wait_ge(stored, 16 * NG)

        @block.gpsimd
        def _(pool):
            G = Count(pool, gstep)
            G.did(pool.memset(ident[:, :], 0.0))
            G.did(pool.memset(ones[:, :], 1.0))
            G.settle()
            for t, fill in ((ident[:, :], 1.0),):
                pool.affine_select(out=t, in_=t, compare_op=ALU.not_equal, fill=fill, base=0,
                                   pattern=[[-1, P]], channel_multiplier=1).then_inc(consts, 1)
            pool.memset(zero, 0.0)
            pool.memset(MB, 0.0)
            pool.memset(rwp[:, :, :], 0.0).then_inc(consts, 1)
            pool.wait_ge(consts, 2)
            G.did(pool.memset(same[:, :], 0.0))
            G.did(pool.memset(ione[:, 0:31], 1))
            G.did(pool.memset(ione[:, 31:32], 0))
            G.did(pool.memset(ish[:, 31:32], 0))
            G.did(pool.iota(ish[:, 0:31].bitcast(I32), [[-1, 31]], base=30, channel_multiplier=0))
            G.did(pool.iota(srow[:, :], [[1, CAP]], base=0, channel_multiplier=0, allow_small_or_imprecise_dtypes=True))
            G.step(pool.iota(scol[:, :], [[P, 2]], base=0, channel_multiplier=1, allow_small_or_imprecise_dtypes=True))
            for d in range(-(NCH - 1), NCH):
                G.step(pool.affine_select(out=same[:, :], in_=same[:, :], compare_op=ALU.not_equal, fill=1.0, base=-NE * d,
                                          pattern=[[-1, P]], channel_multiplier=1))
            G.did(pool.affine_select(out=before[:, :], in_=same[:, :], compare_op=ALU.is_gt, fill=0.0, base=0,
                                     pattern=[[1, P]], channel_multiplier=-1))
            G.step(pool.tensor_copy(differ[:, :], ident[:, :]))
            pool.affine_select(out=differ[:, :], in_=differ[:, :], compare_op=ALU.not_equal, fill=-1.0, base=-1,
                               pattern=[[-1, P]], channel_multiplier=1).then_inc(consts, 1)
            b8 = B8[:, :].rearrange("p (j e) -> p j e", e=HD)
            G.step(pool.affine_select(out=causal[:, :], in_=ones[:, :], compare_op=ALU.is_ge, fill=0.0, base=0,
                                      pattern=[[1, P]], channel_multiplier=-1))
            G.step(pool.affine_select(out=b8, in_=ones[:, :].rearrange("p (j e) -> p j e", e=HD), compare_op=ALU.is_ge, fill=0.0,
                                      base=0, pattern=[[-HD, P // HD], [0, HD]], channel_multiplier=1))
            pool.affine_select(out=b8, in_=b8, compare_op=ALU.is_ge, fill=0.0, base=HD - 1,
                               pattern=[[HD, P // HD], [0, HD]], channel_multiplier=-1).then_inc(consts, 1)
            pool.wait_ge(proj_used, NK)
            pool.wait_ge(projected, NK)
            lo = 0
            A = av
            for lv in range(1, LEVELS):
                n = LT >> lv
                B = lev[:, :, lo:lo + n]
                lo += n
                t1 = xT[:, 0:2 * n].rearrange("p (c t) -> p c t", c=2)
                t2 = xT[:, 2 * n:4 * n].rearrange("p (c t) -> p c t", c=2)
                even, odd = A[:, :, 0::2], A[:, :, 1::2]
                G.did(pool.tensor_tensor(t1, odd[:, 0:1, :].to_broadcast([P, 2, n]), even, ALU.mult))
                G.step(pool.tensor_tensor(t2, odd[:, 1:2, :].to_broadcast([P, 2, n]), even, ALU.mult))
                pool.tensor_tensor(B[:, 0, :], t1[:, 0, :], t2[:, 1, :], ALU.subtract).then_inc(lev_ready, 1)
                pool.tensor_tensor(B[:, 1, :], t1[:, 1, :], t2[:, 0, :], ALU.add).then_inc(lev_ready, 1)
                pool.wait_ge(lev_ready, 2 * lv)
                A = B

            def feed(f):
                pool.wait_ge(tab_stored, 16 * 4 * (f + 1))
                pool.wait_ge(zeroed, 16 * NG * 4)

                def gather(e):
                    if e == 0:
                        pool.wait_ge(idx_ready, f + 1)
                    if e >= RX:
                        pool.wait_ge(y_ready, f * NE + e - RX + 1)
                    for h in range(2):
                        i = h * NE + e
                        pool.indirect_dma_start(out=XE[:, e % RX, h, :], out_offset=None, in_=tab[f],
                                                in_offset=bass.IndirectOffsetOnAxis(ap=idx[:, i:i + 1], axis=0)
                                                ).then_inc(xe_in[e % RX], 16)

                for e in range(RX - 1):
                    gather(e)
                for e in range(NE):
                    if e + RX - 1 < NE:
                        gather(e + RX - 1)
                    pool.wait_ge(y_ready, f * NE + e + 1)
                    if f * NE + e >= 2:
                        pool.wait_ge(scattered[e % 2], 32 * ((f * NE + e) // 2))
                    for h in range(2):
                        i = h * NE + e
                        pool.indirect_dma_start(out=acc[f][e % 2], out_offset=bass.IndirectOffsetOnAxis(ap=idx[:, i:i + 1], axis=0),
                                                in_=yv[:, e % 2, h, :], in_offset=None, compute_op=ALU.add
                                                ).then_inc(scattered[e % 2], 16)

            feed(0)
            pool.wait_ge(x_ready, NG)
            pool.memset(vpad, 0.0).then_inc(vpad_zero, 1)
            feed(1)

        @block.scalar
        def _(act):
            act.wait_ge(inv_in, 16 * 8)
            nc.scalar.activation(Zm[:, :], Rm[:, :], ACT.Square, accum_out=nrm[:, 0:1]).then_inc(nw_sq, 1)

            def root(run):
                act.wait_ge(vp_ready, run + 1)
                nc.scalar.activation(s_rt, s_vp, ACT.Sqrt).then_inc(root_ready, 1)

            def keep_xT(run, n, g):
                act.wait_ge(transposed, run * NG + n + 1)
                nc.scalar.activation(xT[:, g * GW:(g + 1) * GW], ps[:, 6 + n % 2, :], ACT.Copy).then_inc(xT_ready, 1)

            root(0)

            def squares(k):
                act.wait_ge(projected, k + 1)
                if k >= 1:
                    act.wait_ge(mag_ready, k)
                for q in range(4):
                    last = nc.scalar.activation(sq[:, q, :], ps[:, q, :], ACT.Square)
                last.then_inc(squared, 1)
                nc.scalar.activation(av[:, :, k * GW:(k + 1) * GW], ps[:, 0:2, :], ACT.Copy)
                nc.scalar.activation(XC[:, :, 1 + k * GW:1 + (k + 1) * GW], ps[:, 2:4, :], ACT.Copy).then_inc(raw_ready, 1)
                act.wait_ge(mag_ready, k + 1)
                if k >= 1:
                    act.wait_ge(proj_used, k)
                nc.scalar.activation(rt2, mag, ACT.Sqrt).then_inc(rooted, 1)

            for k in range(NK):
                if k >= 1:
                    squares(k - 1)
                for b in range(NB):
                    keep_xT(0, 2 * k + b, b * NK + k)
            squares(NK - 1)

            def feed(f):
                run = 1 + 2 * f
                root(run)
                act.wait_ge(fb_in, 16 * (2 + NCH))
                for n in range(NG):
                    act.wait_ge(transposed, run * NG + n + 1)
                    nc.scalar.activation(xT[:, n * GW:(n + 1) * GW], ps[:, 6 + n % 2, :], ACT.Copy, scale=nwc[:, 0:1]
                                         ).then_inc(xT_ready, 1)
                act.wait_ge(exp_in, f + 1)
                nc.scalar.activation(exs, exs, ACT.Exp).then_inc(exped, 1)
                for e in range(NE):
                    n = f * NE + e
                    act.wait_ge(h_prod, n + 1)
                    if n >= 2:
                        act.wait_ge(y_prod, n - 1)
                    for t in range(FT):
                        last = nc.scalar.activation(hT[:, e % 2, t, :],
                                                    ps[:, 2 * (e % 2) + t // 2, (t % 2) * CAP:(t % 2 + 1) * CAP],
                                                    ACT.Gelu, bias=b1[:, e, t:t + 1])
                    last.then_inc(h_ready, 1)

            feed(0)
            root(2)
            act.wait_ge(vpad_zero, 1)
            act.wait_ge(b8_ready, 1)
            for n in range(NG):
                r = n % 2
                act.wait_ge(transposed, 2 * NG + n + 1)
                nc.scalar.activation(xT[:, n * GW:(n + 1) * GW], ps[:, 6, :], ACT.Copy).then_inc(xT_ready, 1)
                act.wait_ge(q_min, n + 1)
                nc.scalar.activation(exq, exq, ACT.Exp).then_inc(q_exp, 1)
                act.wait_ge(k_min, n + 1)
                nc.scalar.activation(exk, exk, ACT.Exp).then_inc(k_exp, 1)
                act.wait_ge(v_prod, n + 1)
                if n >= 2:
                    act.wait_ge(num_prod, TPG * (n - 1))
                nc.scalar.activation(vn[:, r, :], ps[:, 7, :], ACT.Copy)
                src = ps[:, 7, :].rearrange("p (a i e) -> p a i e", i=4, e=HD)
                dst = vpad[:, r, :, :].rearrange("p t (o i n) -> p (t o) i n", o=4, i=4)
                for i in range(4):
                    last = nc.scalar.activation(dst[:, :, i, HD * i:HD * i + HD], src[:, :, i, :], ACT.Copy)
                last.then_inc(v_ready, 1)
                act.wait_ge(q_ready, n + 1)
                if n >= 2:
                    act.wait_ge(sc_prod, 4 * TPG * (n - 1))
                for i in range(4):
                    last = nc.scalar.activation(Q4[:, r, i, :], qn[:, r, :], ACT.Copy, scale=rowm[:, i:i + 1])
                last.then_inc(q4_ready, 1)
                act.wait_ge(kt_prod, n + 1)
                nc.scalar.activation(kt[:, r, :], ps[:, 6, :], ACT.Copy).then_inc(kt_ready, 1)
            feed(1)

        @block.tensor
        def _(pe):
            pe.wait_ge(consts, 1)

            def transposes(run, n, tiles):
                pe.wait_ge(normed, run * NG + n + 1)
                if run * NG + n >= 2:
                    pe.wait_ge(xT_ready, run * NG + n - 1)
                for t in range(TPG):
                    last = nc.tensor.transpose(ps[:, 6 + n % 2, t * P:(t + 1) * P], tiles(t), ident[:, :])
                last.then_inc(transposed, 1)

            pe.wait_ge(nw_sq, 1)
            nc.tensor.matmul(ps[:, 5, 0:1], ones[:, :], nrm[:, 0:1], start=True, stop=True).then_inc(nw_norm, 1)
            done = [0]

            def inverse(upto):
                while done[0] < min(upto, HALVES):
                    i, half = divmod(done[0], 2)
                    if half == 0:
                        pe.wait_ge(nw_new, i + 1)
                        nc.tensor.matmul(ps[:, 5, 0:P], RT[:, :], XX[:, 0, :], start=True, stop=True).then_inc(nw_Y, 1)
                    else:
                        pe.wait_ge(nw_Z, i + 1)
                        nc.tensor.matmul(ps[:, 4, 0:P], XX[:, 1, :], Zm[:, :], start=True, stop=True)
                        nc.tensor.matmul(ps[:, 4, P:2 * P], Zm[:, :], XX[:, 1, :], start=True, stop=True).then_inc(nw_X, 1)
                    done[0] += 1

            for k in range(NK):
                for b in range(NB):
                    inverse(AT_NORM + 2 + AT_STEP * k + b)
                    if k == 0 and b == 0:
                        pe.wait_ge(wab_in, 32)
                    transposes(0, 2 * k + b, lambda t: stage[:, b * TPG + t, :])
                for b in range(NB):
                    pe.wait_ge(xT_ready, 2 * k + b + 1)
                if k >= 1:
                    pe.wait_ge(raw_ready, k)
                for q in range(4):
                    if q == 2:
                        inverse(AT_NORM + 4 + AT_STEP * k)
                    for b in range(NB):
                        last = nc.tensor.matmul(ps[64 * b:64 * b + 64, q, :], waT[:, q, :],
                                                xT[:, (b * NK + k) * GW:(b * NK + k + 1) * GW], start=True, stop=True)
                last.then_inc(projected, 1)
            inverse(HALVES)
            pe.wait_ge(wo_in, 16 * (2 + 4))
            pe.wait_ge(xT_ready, NG)
            nc.tensor.matmul(ps[:, 6, 0:D], VV[:, 0:2, :].rearrange("p a b -> p (a b)"), MB[0:64, 2, 0, :], start=True, stop=True)
            nc.tensor.matmul(ps[:, 6, D:2 * D], VV[:, 2:4, :].rearrange("p a b -> p (a b)"), MB[0:64, 2, 0, :],
                             start=True, stop=True).then_inc(mt_prod, 1)
            pe.wait_ge(bd_ready, 1)
            pe.wait_ge(h0_in, 16 * 4)
            pe.wait_ge(mt_ready, 1)
            for k in range(NK):
                bank = 4 + 2 * (k % 2)
                if k >= 2:
                    pe.wait_ge(u_used, k - 1)
                pe.wait_ge(proj_used, k + 1)
                xr, xi = XC[:, 0, k * GW:(k + 1) * GW], XC[:, 1, k * GW:(k + 1) * GW]
                nc.tensor.matmul(ps[:, bank, :], BD[:, 0, :], xr, start=True, stop=False)
                nc.tensor.matmul(ps[:, bank, :], BD[:, 2, :], xi, start=False, stop=True)
                nc.tensor.matmul(ps[:, bank + 1, :], BD[:, 1, :], xr, start=True, stop=False)
                nc.tensor.matmul(ps[:, bank + 1, :], BD[:, 0, :], xi, start=False, stop=True).then_inc(u_ready, 1)
            for n in range(2 * NK):
                pe.wait_ge(s_ready, 1 if n < NK else 2)
                if n >= 4:
                    pe.wait_ge(x1_ready, n - 3)
                for t in range(2):
                    at = (2 * n + t) * P
                    for i, lhs in enumerate((SS[:, 0, at:at + P], SS[:, 1, at:at + P], XC[:, 0, at + 1:at + 1 + P])):
                        last = nc.tensor.matmul(ps[:, n % 4, t * 2 * D:(t + 1) * 2 * D], lhs,
                                                MB[:, i, :, :].rearrange("p b d -> p (b d)"), start=(i == 0), stop=(i == 2))
                last.then_inc(ao_ready, 1)

            def feed(f):
                run = 1 + 2 * f
                for n in range(NG):
                    transposes(run, n, lambda t: tb[:, n * TPG + t, 0:D])
                pe.wait_ge(router_in, 32)
                pe.wait_ge(xT_ready, run * NG + NG)
                for i in range(2):
                    for c in range(4):
                        g = 2 * c + i
                        last = nc.tensor.matmul(ps[32 * c:32 * c + 32, 0, :], rwp[:, i, :], xT[:, g * GW:(g + 1) * GW],
                                                start=(i == 0), stop=(i == 1), skip_group_check=True)
                last.then_inc(logit_prod, 1)
                pe.wait_ge(logit_ready, f + 1)
                for q in range(TPG):
                    last = nc.tensor.transpose(ps[:, 1, q * P:(q + 1) * P], L[:, q * P:(q + 1) * P], ident[:, :])
                last.then_inc(logit_T, 1)
                def total(r):
                    pe.wait_ge(counted, r + (f * NCOUNT + 1))
                    nc.tensor.matmul(ps[:, 2, 0:1], same[:, :], cn[:, 0:1], start=True, stop=True).then_inc(totalled, 1)
                total(0)
                total(1)
                with pe.Fori(0, NR - 2, BITS) as r:
                    for j in range(BITS):
                        total(r + (j + 2))
                pe.wait_ge(counted, f * NCOUNT + NR + 1)
                nc.tensor.matmul(ps[:, 2, 1:2], same[:, :], cn[:, 1:2], start=True, stop=True)
                nc.tensor.matmul(ps[:, 2, 2:3], before[:, :], cn[:, 2:3], start=True, stop=True).then_inc(totalled, 1)
                pe.wait_ge(counted, f * NCOUNT + NR + 2)
                nc.tensor.matmul(ps[:, 2, 3:4], before[:, :], cn[:, 3:4], start=True, stop=True).then_inc(totalled, 1)
                pe.wait_ge(seg16, f + 1)
                nc.tensor.matmul(ps[:, 3, :], differ[:, :], cs16, start=True, stop=True).then_inc(seg_diff, 1)
                pe.wait_ge(onehot, f + 1)
                for h in range(2):
                    for e in range(NE):
                        last = nc.tensor.matmul(ps[:, 4 + h, e * 32:e * 32 + 32], G16[:, e, h * P:(h + 1) * P],
                                                cd16[:, e * 32:e * 32 + 32], start=True, stop=True)
                last.then_inc(slots_ready, 1)
                pe.wait_ge(idx_ready, f + 1)

                def turn(e):
                    n = f * NE + e
                    pe.wait_ge(xe_in[e % RX], 32 * (f * NE // RX + e // RX + 1))
                    if n >= 2:
                        pe.wait_ge(xeT_ready, n - 1)
                    for h in range(2):
                        last = nc.tensor.transpose(ps[:, 4 + e % 2, h * P:(h + 1) * P],
                                                   XE[:, e % RX, h, 0:D], ident[:, :])
                    last.then_inc(xe_T, 1)

                turn(0)
                for e in range(NE + 1):
                    n = f * NE + e
                    if e + 1 < NE:
                        turn(e + 1)
                    if e < NE:
                        if e % 4 == 0:
                            pe.wait_ge(wf_in[e // 4], 32)
                        pe.wait_ge(xeT_ready, n + 1)
                        if n >= 2:
                            pe.wait_ge(h_ready, n - 1)
                        for t in range(FT):
                            last = nc.tensor.matmul(ps[:, 2 * (e % 2) + t // 2, (t % 2) * CAP:(t % 2 + 1) * CAP],
                                                    f1w[:, e, t * P:(t + 1) * P], xeT[:, e % 2, :], start=True, stop=True)
                        last.then_inc(h_prod, 1)
                    if e >= 1:
                        m = e - 1
                        pe.wait_ge(h_ready, n)
                        if n - 1 >= 2:
                            pe.wait_ge(y_ready, n - 2)
                        for h in range(2):
                            for t in range(FT):
                                last = nc.tensor.matmul(ps[:, 6 + m % 2, h * P:(h + 1) * P], hT[:, m % 2, t, h * P:(h + 1) * P],
                                                        f2w[:, m, t, :], start=(t == 0), stop=(t == FT - 1))
                        last.then_inc(y_prod, 1)

            feed(0)

            def use(i, n):
                r, cols = n % 2, slice(n * GW, (n + 1) * GW)
                if i == 0:
                    pe.wait_ge(normed, 2 * NG + n + 1)
                    if n == 0:
                        pe.wait_ge(x_ready, NG)
                    else:
                        pe.wait_ge(kt_ready, n)
                    for t in range(TPG):
                        last = nc.tensor.transpose(ps[:, 6, t * P:(t + 1) * P], stage[:, r * TPG + t, :], ident[:, :])
                    last.then_inc(transposed, 1)
                if i == 1:
                    pe.wait_ge(wb_in, 32)
                    pe.wait_ge(xT_ready, 2 * NG + n + 1)
                    if n >= 2:
                        pe.wait_ge(x3_ready, n - 1)
                    elif n == 1:
                        pe.wait_ge(den_ready, 1)
                    nc.tensor.matmul(ps[:, 7, :], wqkv[:, 0, :], xT[:, cols], start=True, stop=True).then_inc(q_prod, 1)
                if i == 2:
                    nc.tensor.matmul(ps[:, 6, :], wqkv[:, 1, :], xT[:, cols], start=True, stop=True).then_inc(k_prod, 1)
                if i == 3:
                    pe.wait_ge(q_ready, n + 1)
                    for t in range(TPG):
                        c0 = n * GW + t * P
                        last = nc.tensor.matmul(ps[:, 7, t * P:(t + 1) * P], xT[:, c0:c0 + P], wqkv[:, 2, :], start=True, stop=True)
                    last.then_inc(v_prod, 1)
                if i == 4:
                    pe.wait_ge(k_ready, n + 1)
                    for t in range(TPG):
                        last = nc.tensor.transpose(ps[:, 6, t * P:(t + 1) * P], kT[:, r, t * P:(t + 1) * P], ident[:, :])
                    last.then_inc(kt_prod, 1)
                if i == 5:
                    pe.wait_ge(qz_ready, n + 1)
                    pe.wait_ge(v_ready, n + 1)
                    nc.tensor.matmul(ps[:, 7, :], B8[:, :], Zc, start=True, stop=True).then_inc(den_prod, 1)

            def scores(T):
                n, t = divmod(T, TPG)
                r = n % 2
                pe.wait_ge(q4_ready, n + 1)
                for o in range(4):
                    if T >= 1:
                        pe.wait_ge(sc_masked, 4 * (T - 1) + o + 1)
                    q = slice(32 * o, 32 * o + 32)
                    nc.tensor.matmul(ps[:, o, :], kT[q, r, t * P:(t + 1) * P], Q4[q, r, :, t * P:(t + 1) * P],
                                     start=True, stop=True, tile_position=(32 * o, 0)).then_inc(sc_prod, 1)

            def numerator(T):
                n, t = divmod(T, TPG)
                r, bank, first = n % 2, 4 + T % 2, T % (NT // NB) == 0
                cols = slice(t * P, (t + 1) * P)
                pe.wait_ge(kt_ready, n + 1)
                pe.wait_ge(v_ready, n + 1)
                pe.wait_ge(sc_masked, 4 * (T + 1))
                if T >= 2:
                    pe.wait_ge(num_used, T - 1)
                if not first:
                    pe.wait_ge(s_upd, T)
                    nc.tensor.matmul(ps[:, bank, 0:P], S[:, T % 2, :], qn[:, r, cols], start=True, stop=False, skip_group_check=True)
                for i in range(4):
                    for o in range(4):
                        nc.tensor.matmul(ps[32 * o:32 * o + 32, bank, 0:P], vpad[:, r, t, (4 * o + i) * 32:(4 * o + i + 1) * 32],
                                         att[:, T % 2, o, i * P:(i + 1) * P], start=(first and i == 0), stop=(i == 3),
                                         skip_group_check=True)
                nc.tensor.matmul(ps[:, bank, P:2 * P], kt[:, r, cols], vn[:, r, cols], start=True, stop=True,
                                 skip_group_check=True).then_inc(num_prod, 1)

            pe.wait_ge(consts, 4)
            for i in range(6):
                use(i, 0)
            scores(0)
            for T in range(NT):
                n, t = divmod(T, TPG)
                if T + 1 < NT and t < 3:
                    scores(T + 1)
                if n + 1 < NG and t < 3:
                    use(2 * t, n + 1)
                    use(2 * t + 1, n + 1)
                if T + 1 < NT and t == 3:
                    scores(T + 1)
                numerator(T)
                if t == 3:
                    pe.wait_ge(num_used, T + 1)
                    if n + 1 < NG:
                        pe.wait_ge(den_ready, n + 2)
                    for j in range(TPG):
                        last = nc.tensor.matmul(ps[:, 7, j * P:(j + 1) * P], On[:, n % 2, j * P:(j + 1) * P], wou[:, :],
                                                start=True, stop=True)
                    last.then_inc(fin_prod, 1)
            feed(1)

        @block.vector
        def _(dve):
            V = Count(dve, dstep)

            def tt(o, a, b, op):
                return nc.vector.tensor_tensor(o, a, b, op)

            def ts(o, a, s1, s2, op0, op1=None, **kw):
                if op1 is None:
                    return nc.vector.tensor_scalar(o, a, s1, s2, op0, **kw)
                return nc.vector.tensor_scalar(o, a, s1, s2, op0, op1, **kw)

            def stt(o, a, s, b, op0, op1, **kw):
                return nc.vector.scalar_tensor_tensor(o, a, s, b, op0, op1, **kw)

            def stats(g):
                for t in range(TPG):
                    V.did(nc.vector.bn_stats(bst[:, g * TPG + t, :], xs[:, g * TPG + t, :]))

            def scales(run, mul, eps, between=lambda: None):
                V.settle()
                V.did(tt(s_d, bst[:, :, 1], bst[:, :, 4], ALU.subtract))
                V.did(tt(s_w, bst[:, :, 2], bst[:, :, 5], ALU.add))
                V.step(tt(s_mean, bst[:, :, 1], bst[:, :, 4], ALU.add))
                V.did(nc.vector.tensor_scalar(s_mean, s_mean, 0.5, None, ALU.mult))
                V.step(tt(s_d, s_d, s_d, ALU.mult))
                V.step(nc.vector.scalar_tensor_tensor(s_w, s_d, P / 4.0, s_w, ALU.mult, ALU.add))
                nc.vector.tensor_scalar(s_vp, s_w, mul / P, eps, ALU.mult, ALU.add).then_inc(vp_ready, 1)
                between()
                dve.wait_ge(root_ready, run + 1)
                V.step(nc.vector.reciprocal(s_r, s_rt))
                V.step(tt(s_q, s_r, s_r, ALU.mult))
                V.step(tt(s_q, s_q, s_vp, ALU.mult))
                V.step(nc.vector.tensor_scalar(s_q, s_q, -0.5, 1.5, ALU.mult, ALU.add))
                V.step(tt(s_r, s_r, s_q, ALU.mult))

            def normalise(run, n, g, dst):
                for t in range(TPG):
                    j = g * TPG + t
                    last = nc.vector.tensor_scalar(dst(t), xs[:, j, :], s_mean[:, j:j + 1], s_r[:, j:j + 1],
                                                   ALU.subtract, ALU.mult)
                last.then_inc(normed, 1)

            dve.wait_ge(inv_in, 16 * 8)
            dve.wait_ge(nw_sq, 1)
            dve.wait_ge(consts, 1)
            V.did(nc.vector.memset(BD[:, :, :], 0.0))
            V.did(nc.vector.tensor_scalar(Rm[0:64, 64:128], Rm[0:64, 64:128], -1.0, None, ALU.mult))
            V.did(nc.vector.tensor_scalar(RT[64:128, 0:64], RT[64:128, 0:64], -1.0, None, ALU.mult))
            V.did(nc.vector.tensor_scalar(aI[:, 0, :], ident[:, :], WA / WB, None, ALU.mult))
            V.did(nc.vector.tensor_scalar(aI[:, 1, :], ident[:, :], 2.0, None, ALU.mult))
            dve.wait_ge(nw_norm, 1)
            V.step(nc.vector.tensor_scalar(nrm[:, 1:2], ps[:, 5, 0:1], 0.5, None, ALU.mult))
            V.step(nc.vector.reciprocal(nrm[:, 2:3], nrm[:, 1:2]))
            nc.vector.tensor_scalar(XX[:, 0, :], RT[:, :], nrm[:, 2:3], None, ALU.mult)
            nc.vector.tensor_scalar(XX[:, 1, :], Rm[:, :], nrm[:, 2:3], None, ALU.mult).then_inc(nw_new, 1)
            done = [0]

            def inverse(n=1):
                for _ in range(n):
                    if done[0] == HALVES:
                        return
                    i, half = divmod(done[0], 2)
                    if half == 0:
                        dve.wait_ge(nw_Y, i + 1)
                        stt(Zm[:, :], ps[:, 5, 0:P], -1.0, aI[:, 0 if i < N_WIDE else 1, :], ALU.mult, ALU.add).then_inc(nw_Z, 1)
                    else:
                        dve.wait_ge(nw_X, i + 1)
                        ts(XX[:, :, :].rearrange("p a b -> p (a b)"), ps[:, 4, 0:2 * P], WB if i < N_WIDE else 1.0, None, ALU.mult
                           ).then_inc(nw_new, 1)
                    done[0] += 1

            order = [b * NK + k for k in range(NK) for b in range(NB)]
            for g in order:
                dve.wait_ge(x_in[g], 16)
                stats(g)
                inverse()
            scales(0, 1.0, EPS, lambda: inverse())
            inverse(AT_NORM - done[0])
            assert done[0] == AT_NORM

            def norm_a(k):
                for b in range(NB):
                    n = 2 * k + b
                    if n >= 2:
                        dve.wait_ge(transposed, n - 1)
                    normalise(0, n, b * NK + k, lambda t: stage[:, b * TPG + t, :])
                    inverse()

            def coefficients(k):
                assert done[0] >= min(HALVES, AT_NORM + 4 + AT_STEP * k), (done[0], k)
                dve.wait_ge(squared, k + 1)
                if k >= 1:
                    dve.wait_ge(rooted, k)
                nc.vector.tensor_tensor(mag, sq[:, 0:4:2, :], sq[:, 1:4:2, :], ALU.add).then_inc(mag_ready, 1)
                inverse()
                dve.wait_ge(mag_ready, k + 1)
                V.step(nc.vector.tensor_scalar(rec, mag[:, 0, :], 1.0, None, ALU.add))
                V.step(nc.vector.reciprocal(rec, rec))
                inverse()
                dve.wait_ge(rooted, k + 1)
                dve.wait_ge(raw_ready, k + 1)
                X = XC[:, :, 1 + k * GW:1 + (k + 1) * GW]
                V.did(tt(X, X, rt2[:, 1:2, :].to_broadcast([P, 2, GW]), ALU.mult))
                inverse()
                V.step(tt(rec, rec, rt2[:, 0, :], ALU.mult))
                A = av[:, :, k * GW:(k + 1) * GW]
                tt(A, A, rec.rearrange("p (a t) -> p a t", a=1).to_broadcast([P, 2, GW]), ALU.mult).then_inc(proj_used, 1)
                inverse()

            norm_a(0)
            for k in range(NK):
                if k + 1 < NK:
                    norm_a(k + 1)
                inverse(min(HALVES, AT_COEF + AT_STEP * k) - done[0])
                coefficients(k)
            inverse(HALVES)
            dve.wait_ge(nw_new, N_WIDE + N_LAST + 1)
            lo_, hi_ = slice(0, 64), slice(64, 128)
            V.did(nc.vector.tensor_copy(BD[lo_, 0, lo_], XX[lo_, 1, lo_]))
            V.did(nc.vector.tensor_copy(BD[hi_, 0, hi_], XX[hi_, 1, hi_]))
            V.did(nc.vector.tensor_copy(BD[lo_, 1, lo_], XX[lo_, 1, hi_]))
            V.did(nc.vector.tensor_scalar(BD[hi_, 1, hi_], XX[hi_, 1, lo_], -1.0, None, ALU.mult))
            V.did(nc.vector.tensor_scalar(BD[lo_, 2, lo_], XX[lo_, 1, hi_], -1.0, None, ALU.mult))
            nc.vector.tensor_copy(BD[hi_, 2, hi_], XX[hi_, 1, lo_]).then_inc(bd_ready, 1)
            dve.wait_ge(mt_prod, 1)
            for b, r in enumerate((lo_, hi_)):
                V.did(nc.vector.tensor_copy(MB[r, 0, b, :], ps[r, 6, 0:D]))
                last = nc.vector.tensor_scalar(MB[r, 1, b, :], ps[r, 6, D:2 * D], -1.0, None, ALU.mult)
            last.then_inc(mt_ready, 1)

            def times(cr, ci, n, q, o, add_to):
                t1, t2 = T1[:, :, 0:n], T2[:, :, 0:n]
                V.did(tt(t1, cr.to_broadcast([P, 2, n]), q, ALU.mult))
                V.step(tt(t2, ci.to_broadcast([P, 2, n]), q, ALU.mult))
                to = t1 if add_to else o
                if add_to:
                    V.did(tt(t1[:, 0, :], t1[:, 0, :], t2[:, 1, :], ALU.subtract))
                    V.step(tt(t1[:, 1, :], t1[:, 1, :], t2[:, 0, :], ALU.add))
                    V.step(tt(o, o, t1, ALU.add))
                else:
                    V.did(tt(to[:, 0, :], t1[:, 0, :], t2[:, 1, :], ALU.subtract))
                    V.step(tt(to[:, 1, :], t1[:, 1, :], t2[:, 0, :], ALU.add))

            for k in range(NK):
                H = GW // 2
                dve.wait_ge(u_ready, k + 1)
                dve.wait_ge(proj_used, k + 1)
                e, o = slice(k * GW, (k + 1) * GW, 2), slice(k * GW + 1, (k + 1) * GW, 2)
                U = ps[:, 4 + 2 * (k % 2):6 + 2 * (k % 2), :]
                times(av[:, 0:1, e], av[:, 1:2, e], H, U[:, :, 0::2], SS[:, :, e], False)
                v = mag[:, :, 0:H]
                tt(v, SS[:, :, e], U[:, :, 1::2], ALU.add).then_inc(u_used, 1)
                dve.wait_ge(u_used, k + 1)
                times(av[:, 0:1, o], av[:, 1:2, o], H, v, SS[:, :, o], False)
            lv_at = [0] * (LEVELS + 1)
            for lv in range(2, LEVELS):
                lv_at[lv] = lv_at[lv - 1] + (LT >> (lv - 1))
            for lv in range(1, LEVELS):
                s, n = 1 << lv, LT >> (lv + 1)
                dve.wait_ge(lev_ready, 2 * lv)
                A = lev[:, :, lv_at[lv]:lv_at[lv] + 2 * n]
                for c0 in range(0, n, GW):
                    w = min(GW, n - c0)
                    q = SS[:, :, s - 1 + c0 * 2 * s::2 * s][:, :, 0:w]
                    o = SS[:, :, 2 * s - 1 + c0 * 2 * s::2 * s][:, :, 0:w]
                    times(A[:, 0:1, 2 * c0 + 1::2][:, :, 0:w], A[:, 1:2, 2 * c0 + 1::2][:, :, 0:w], w, q, o, True)
            for lv in range(LEVELS - 2, -1, -1):
                s, n = 1 << lv, (LT >> (lv + 1)) - 1
                A = lev[:, :, lv_at[lv]:lv_at[lv] + 2 * (n + 1)] if lv else av
                for c0 in range(0, n, GW):
                    w = min(GW, n - c0)
                    q = SS[:, :, 2 * s - 1 + c0 * 2 * s::2 * s][:, :, 0:w]
                    o = SS[:, :, 3 * s - 1 + c0 * 2 * s::2 * s][:, :, 0:w]
                    times(A[:, 0:1, 2 * c0 + 2::2][:, :, 0:w], A[:, 1:2, 2 * c0 + 2::2][:, :, 0:w], w, q, o, True)
                    if lv == 0:
                        nc.vector.tensor_copy(nrm[:, 3:4], nrm[:, 2:3]).then_inc(s_ready, 1)
            for n in range(2 * NK):
                dve.wait_ge(ao_ready, n + 1)
                row = xs[:, :, :].rearrange("p (b j) d -> p b j d", b=NB)[:, :, 2 * n:2 * n + 2, :]
                tt(row, row, ps[:, n % 4, :].rearrange("p (t b d) -> p b t d", t=2, b=NB), ALU.add).then_inc(x1_ready, 1)
                dve.wait_ge(x1_ready, n + 1)
                for j in (2 * n, 2 * n + 1, NT // 2 + 2 * n, NT // 2 + 2 * n + 1):
                    V.did(nc.vector.bn_stats(bst[:, j, :], xs[:, j, :]))

            def feed(f):
                run = 1 + 2 * f
                scales(run, 1.0 + EPS, EPS * EPS)
                dve.wait_ge(zeroed, 16 * NG * 4)
                for g in range(NG):
                    normalise(run, g, g, lambda t: tb[:, g * TPG + t, 0:D])
                dve.wait_ge(logit_prod, f + 1)
                ts(L, ps[:, 0, :], rbc[:, 0:1], None, ALU.add).then_inc(logit_ready, 1)
                dve.wait_ge(logit_T, f + 1)
                lt = ps[:, 1, :].rearrange("p (t e) -> p t e", e=NE)
                ex = exs.rearrange("p (t e) -> p t e", e=NE)

                def over(v):
                    return v.rearrange("p (t e) -> p t e", e=1).to_broadcast([P, NT, NE])
                V.step(nc.vector.tensor_reduce(smx, lt, AX.X, ALU.max))
                tt(ex, lt, over(smx), ALU.subtract).then_inc(exp_in, 1)
                M, cand, neg, thr, lo, hi = (tku[:, i:i + 1] for i in range(6))
                basis, flip = tku[:, 10:11], tku[:, 11:12]
                junk = gt
                base = f * NCOUNT
                dve.wait_ge(consts, 3)
                if f == 0:
                    V.step(tt(bits[:, 0:32], ione[:, :], ish[:, :], ALU.logical_shift_left))
                ts(junk, L, 0.0, None, ALU.is_ge, ALU.add, accum_out=cn[:, 0:1]).then_inc(counted, 1)
                dve.wait_ge(exped, f + 1)
                V.step(nc.vector.tensor_reduce(smx, ex, AX.X, ALU.add))
                V.step(nc.vector.reciprocal(smx, smx))
                for q in range(TPG):
                    prob = tt(tb[:, q::TPG, D:TW], ex[:, q * NCH:(q + 1) * NCH, :], over(smx)[:, q * NCH:(q + 1) * NCH, :], ALU.mult)
                prob.then_inc(tab_ready, 1)
                dve.wait_ge(totalled, base + 1)
                V.step(ts(neg, ps[:, 2, 0:1], CAP - 0.5, None, ALU.is_lt))
                V.step(ts(M, neg, 31, None, ALU.logical_shift_left))
                V.did(tt(cand, M, bits[:, 0:1], ALU.bitwise_or))
                V.step(tt(nb[:, 0:32], bits[:, 0:32], neg.to_broadcast([P, 32]), ALU.mult))
                def bit(r, at):
                    ts(junk, L, cand.bitcast(F32), None, ALU.is_ge, ALU.add, accum_out=cn[:, 0:1]).then_inc(counted, 1)
                    tt(basis, M, nb[:, bass.ds(r, 1)], ALU.bitwise_or).then_inc(cand_ready, 1)
                    dve.wait_ge(totalled, at + (base + 2))
                    stt(flip, ps[:, 2, 0:1], CAP - 0.5, bits[:, bass.ds(r, 1)], ALU.is_ge, ALU.mult).then_inc(cand_ready, 1)
                    dve.wait_ge(cand_ready, at * 4 + (f * 4 * (NR - 1) + 2))
                    stt(cand, basis, flip, bits[:, bass.ds(r + 1, 1)], ALU.bitwise_xor, ALU.bitwise_or).then_inc(cand_ready, 1)
                    tt(M, basis, flip, ALU.bitwise_xor).then_inc(cand_ready, 1)
                    dve.wait_ge(cand_ready, at * 4 + (f * 4 * (NR - 1) + 4))
                bit(0, 0)
                with dve.Fori(0, NR - 2, BITS) as r:
                    for j in range(BITS):
                        bit(r + (j + 1), r + (j + 1))
                V.did(ts(lo, M, 0xFFFF, None, ALU.bitwise_and))
                V.step(ts(hi, M, 16, None, ALU.logical_shift_right))
                V.step(tt(lo, lo, neg, ALU.add))
                V.step(ts(cand, lo, 16, None, ALU.logical_shift_right))
                V.step(tt(hi, hi, cand, ALU.add))
                V.did(ts(lo, lo, 0xFFFF, None, ALU.bitwise_and))
                V.step(ts(hi, hi, 16, None, ALU.logical_shift_left))
                V.step(tt(thr, hi, lo, ALU.bitwise_or))
                T = thr.bitcast(F32)
                V.did(ts(gt, L, T, None, ALU.is_gt, ALU.add, accum_out=cn[:, 1:2]))
                ts(eq, L, T, None, ALU.is_equal, ALU.add, accum_out=cn[:, 2:3]).then_inc(counted, 1)
                dve.wait_ge(counted, base + NR + 1)
                V.did(nc.vector.tensor_tensor_scan(cnt, eq, eq, 0.0, ALU.add, ALU.max))
                dve.wait_ge(totalled, base + NR + 1)
                need = tk[:, 8:9]
                V.step(ts(need, ps[:, 2, 1:2], -1.0, float(CAP), ALU.mult, ALU.add))
                V.step(tt(need, need, ps[:, 2, 2:3], ALU.subtract))
                V.step(stt(eq, cnt, need, eq, ALU.is_le, ALU.mult))
                stt(gt, eq, 0.0, gt, ALU.add, ALU.add, accum_out=cn[:, 3:4]).then_inc(counted, 1)
                dve.wait_ge(counted, base + NR + 2)
                dve.wait_ge(totalled, base + NR + 2)
                V.step(nc.vector.tensor_copy(tk[:, 9:10], ps[:, 2, 3:4]))
                nc.vector.tensor_tensor_scan(cnt, gt, gt, tk[:, 9:10], ALU.add, ALU.max).then_inc(cnt_ready, 1)
                dve.wait_ge(seg_in, 16 * NCH * (f + 1))
                nc.vector.tensor_copy(cs16, csg).then_inc(seg16, 1)
                end = csg.rearrange("p (e t) -> p e t", e=NE)[:, :, 31:32].to_broadcast([P, NE, CAP])
                V.did(tt(G16, srow[:, :].rearrange("p (e s) -> p e s", e=1).to_broadcast([P, NE, CAP]), end, ALU.is_lt))
                dve.wait_ge(seg_diff, f + 1)
                V.step(nc.vector.tensor_copy(cd16, ps[:, 3, :]))
                nc.vector.memset(cd16.rearrange("p (e t) -> p e t", e=NE)[:, :, 31:32], 1.0).then_inc(onehot, 1)
                dve.wait_ge(slots_ready, f + 1)
                lev3 = G16.rearrange("p e s -> p (e s)")[:, 0:2 * NE * 31].rearrange("p (h t) -> p h t", h=2 * NE)
                for h in range(2):
                    V.did(ts(lev3[:, h * NE:(h + 1) * NE, :], ps[:, 4 + h, :].rearrange("p (e t) -> p e t", e=NE)[:, :, 0:31],
                             scol[:, h:h + 1], None, ALU.is_le))
                V.settle()
                V.step(nc.vector.tensor_reduce(lesum, lev3, AX.X, ALU.add))
                col = ps[:, 4:6, :].rearrange("p h (e t) -> p (h e) t", e=NE)[:, :, 31:32]
                V.step(stt(lesum, col.rearrange("p a t -> p (a t)"), -32.0, lesum, ALU.mult, ALU.add))
                ts(idx[:, :], lesum, 32.0 * P, None, ALU.add).then_inc(idx_ready, 1)
                dve.wait_ge(b2_in, 16 * (f + 1))

                def keep_xe(e):
                    n = f * NE + e
                    dve.wait_ge(xe_T, n + 1)
                    if n >= 2:
                        dve.wait_ge(h_prod, n - 1)
                    ts(xeT[:, e % 2, :], ps[:, 4 + e % 2, 0:CAP], nwc[:, 0:1], None, ALU.mult
                       ).then_inc(xeT_ready, 1)

                keep_xe(0)
                for e in range(NE):
                    n = f * NE + e
                    if e + 1 < NE:
                        keep_xe(e + 1)
                    dve.wait_ge(y_prod, n + 1)
                    if n >= 2:
                        dve.wait_ge(scattered[e % 2], 32 * (n // 2))
                    y = yv[:, e % 2, :, :]
                    V.step(tt(y[:, :, 0:D], ps[:, 6 + e % 2, 0:2 * P].rearrange("p (h d) -> p h d", h=2),
                              b2[:, e:e + 1, :].to_broadcast([P, 2, D]), ALU.add))
                    for h in range(2):
                        V.did(ts(y[:, h, 0:D], y[:, h, 0:D], XE[:, e % RX, h, D + e:D + e + 1], None, ALU.mult))
                    nc.vector.tensor_copy(y[:, :, D:AW], XE[:, e % RX, :, D + e:D + e + 1]).then_inc(y_ready, 1)
                for g in range(NG):
                    t = slice(g * TPG, (g + 1) * TPG)
                    dve.wait_ge(acc_in[g], 32 * (f + 1))
                    V.step(tt(tb[:, t, 0:AW], tb[:, t, 0:AW], acc1[:, t, :], ALU.add))
                    gs = tb[:, t, D:AW].rearrange("p t a -> p (t a)")
                    V.step(stt(rinv[:, t], gs, 0.0, gs, ALU.is_equal, ALU.add))
                    V.step(nc.vector.reciprocal(rinv[:, t], rinv[:, t]))
                    for j in range(g * TPG, (g + 1) * TPG):
                        last = stt(xs[:, j, :], tb[:, j, 0:D], rinv[:, j:j + 1], xs[:, j, :], ALU.mult, ALU.add)
                    last.then_inc(x_ready, 1)
                    if f == 0:
                        dve.wait_ge(x_ready, g + 1)
                        stats(g)

            feed(0)
            scales(2, 1.0, EPS)
            nc.vector.tensor_reduce(rowm[:, :], B8[:, :].rearrange("p (o i e) -> p i e o", o=4, i=4)[:, :, 0, :], AX.X, ALU.add
                                    ).then_inc(b8_ready, 1)

            def norm_b(n):
                if n >= 2:
                    dve.wait_ge(transposed, 2 * NG + n - 1)
                normalise(2, n, n, lambda t: stage[:, (n % 2) * TPG + t, :])

            def take_q(n):
                dve.wait_ge(q_prod, n + 1)
                ts(exq, ps[:, 7, :], 0.0, None, ALU.min).then_inc(q_min, 1)
                if n >= 2:
                    dve.wait_ge(num_prod, TPG * (n - 1))
                    dve.wait_ge(q4_ready, n - 1)
                dve.wait_ge(q_exp, n + 1)
                V.step(stt(qn[:, n % 2, :], ps[:, 7, :], 0.0, exq, ALU.max, ALU.add))
                ts(qn[:, n % 2, :], qn[:, n % 2, :], HD ** -0.5, None, ALU.mult).then_inc(q_ready, 1)

            def take_k(n):
                r = n % 2
                dve.wait_ge(k_prod, n + 1)
                ts(exk, ps[:, 6, :], 0.0, None, ALU.min).then_inc(k_min, 1)
                if n % NK:
                    V.step(nc.vector.tensor_copy(zc[:, :], exz[:, GW - 1:GW]))
                dve.wait_ge(k_exp, n + 1)
                stt(kT[:, r, :], ps[:, 6, :], 0.0, exk, ALU.max, ALU.add).then_inc(k_ready, 1)
                dve.wait_ge(k_ready, n + 1)
                V.step(nc.vector.tensor_tensor_scan(exz, kT[:, r, :], kT[:, r, :], zc[:, :] if n % NK else 0.0, ALU.add, ALU.max))
                dve.wait_ge(q_ready, n + 1)
                tt(Zc, exz, qn[:, r, :], ALU.mult).then_inc(qz_ready, 1)

            def take_den(n):
                dve.wait_ge(den_prod, n + 1)
                V.step(ts(rden[:, n % 2, :], ps[:, 7, :], 1e-6, None, ALU.max))
                nc.vector.reciprocal(rden[:, n % 2, :], rden[:, n % 2, :]).then_inc(den_ready, 1)

            def mask(T):
                if T >= 2:
                    dve.wait_ge(num_prod, T - 1)
                for o in range(4):
                    dve.wait_ge(sc_prod, 4 * T + o + 1)
                    tt(att[:, T % 2, o, :].rearrange("p (i l) -> p i l", i=4), ps[:, o, :].rearrange("p (i l) -> p i l", i=4),
                       causal[:, :].rearrange("p (i l) -> p i l", i=1).to_broadcast([P, 4, P]), ALU.mult).then_inc(sc_masked, 1)

            def take_numerator(T):
                n, t = divmod(T, TPG)
                r, bank, cols = n % 2, 4 + T % 2, slice(t * P, (t + 1) * P)
                dve.wait_ge(num_prod, T + 1)
                first = T % (NT // NB) == 0
                V.did(tt(S[:, (T + 1) % 2, :] if first else Stmp, ps[:, bank, P:2 * P], B8[:, :], ALU.mult))
                dve.wait_ge(den_ready, n + 1)
                tt(On[:, r, cols], ps[:, bank, 0:P], rden[:, r, cols], ALU.mult).then_inc(num_used, 1)
                if first:
                    nc.vector.tensor_copy(tk[:, 12:13], tk[:, 13:14]).then_inc(s_upd, 1)
                else:
                    V.settle()
                    dve.wait_ge(s_upd, T)
                    tt(S[:, (T + 1) % 2, :], S[:, T % 2, :], Stmp, ALU.add).then_inc(s_upd, 1)

            def add_out(n):
                dve.wait_ge(fin_prod, n + 1)
                row = xs[:, n * TPG:(n + 1) * TPG, :].rearrange("p t d -> p (t d)")
                tt(row, row, ps[:, 7, :], ALU.add).then_inc(x3_ready, 1)
                dve.wait_ge(x3_ready, n + 1)
                stats(n)

            V.did(nc.vector.memset(tk[:, 13:14], 0.0))
            norm_b(0)
            norm_b(1)
            take_q(0)
            take_k(0)
            take_den(0)
            mask(0)
            for T in range(NT):
                n, t = divmod(T, TPG)
                if T + 1 < NT and t < 3:
                    mask(T + 1)
                if t == 0 and n >= 1:
                    add_out(n - 1)
                if n + 1 < NG:
                    if t == 0:
                        take_q(n + 1)
                    if t == 1:
                        take_k(n + 1)
                    if t == 2:
                        take_den(n + 1)
                        if n + 2 < NG:
                            norm_b(n + 2)
                if T + 1 < NT and t == 3:
                    mask(T + 1)
                take_numerator(T)
            add_out(NG - 1)
            feed(1)


def kernel(**inputs):
    import numpy as np
    import concourse.bacc as bacc
    from concourse.bass_utils import run_bass_kernel_spmd as run

    i = {k[3:]: np.asarray(v) for k, v in inputs.items()}
    inner, dim = i["attn_a_w_out"].shape[1], i["attn_a_w_out"].shape[0]
    E, F, _ = i["ffn_fc1_weight"].shape
    p = 128
    arrays = {
        "x": i["attn_a_x"],
        "wa": i["attn_a_w_a"].reshape(inner, 2, dim).transpose(2, 1, 0),
        "wx": i["attn_a_w_x"].reshape(inner, 2, dim).transpose(2, 1, 0),
        "wo": i["attn_a_w_out"].T,
        "vr": i["attn_a_mat_v_real"], "vi": i["attn_a_mat_v_imag"],
        "vrT": i["attn_a_mat_v_real"].T, "viT": i["attn_a_mat_v_imag"].T,
        "h0r": i["attn_a_last_hidden_real"].reshape(inner, 1), "h0i": i["attn_a_last_hidden_imag"].reshape(inner, 1),
        "wqkvT": i["attn_b_W_qkv"].T, "woutT": i["attn_b_W_out"].T,
        "nw": i["ffn_norm_weight"].reshape(dim, 1),
        "rwT": i["ffn_router_weight"].T, "rb": i["ffn_router_bias"].reshape(E, 1),
        "f1T": i["ffn_fc1_weight"].transpose(2, 0, 1),
        "f1b": i["ffn_fc1_bias"].reshape(E, F // p, p).transpose(2, 0, 1),
        "f2T": i["ffn_fc2_weight"].reshape(E, dim, F // p, p).transpose(3, 0, 2, 1),
        "f2b": i["ffn_fc2_bias"],
    }
    arrays = {k: np.ascontiguousarray(v) for k, v in arrays.items()}
    nc = bacc.Bacc("TRN2", target_bir_lowering=False, num_devices=1)
    args = {k: nc.dram_tensor(f"in_{k}", v.shape, mybir.dt.from_np(v.dtype), kind="ExternalInput").ap() for k, v in arrays.items()}
    args["out"] = nc.dram_tensor("out_0", arrays["x"].shape, F32, kind="ExternalOutput").ap()
    build(nc, **args)
    r = run(nc, [{f"in_{k}": v for k, v in arrays.items()}], core_ids=[0])
    return r.results[0]["out_0"]
```

```python
from contextlib import ExitStack

import concourse.bass as bass
from concourse import mybir

F32 = mybir.dt.float32
BF16 = mybir.dt.bfloat16
F16 = mybir.dt.float16
I32 = mybir.dt.int32
U32 = mybir.dt.uint32
ALU = mybir.AluOpType
ACT = mybir.ActivationFunctionType
AX = mybir.AxisListType

P = 128
EPS = 1e-5


class Count:

    def __init__(self, engine, sem):
        self.engine, self.sem, self.n = engine, sem, 0

    def did(self, instruction):
        instruction.then_inc(self.sem, 1)
        self.n += 1

    def settle(self):
        self.engine.wait_ge(self.sem, self.n)

    def step(self, instruction):
        self.did(instruction)
        self.settle()


def build(nc, x, wa, wx, wo, vr, vi, vrT, viT, h0r, h0i, wqkvT, woutT, nw, rwT, rb, f1T, f1b, f2T, f2b, out):
    NB, LT, D = x.shape
    INNER = vr.shape[0]
    NTOK = NB * LT
    NT = NTOK // P
    TPG = 4
    NG = NT // TPG
    GW = TPG * P
    NK = LT // GW
    LEVELS = LT.bit_length() - 1
    NE = rwT.shape[1]
    NF = f1T.shape[2]
    FT = NF // P
    CAP = NTOK // NE
    TW = D + NE
    AW = D + 1
    NCH = P // NE

    tab = [nc.dram_tensor(f"tab{f}", [NTOK, TW], F32).ap() for f in range(2)]
    acc = [[nc.dram_tensor(f"acc{f}{i}", [NTOK, AW], F32).ap() for i in range(2)] for f in range(2)]
    cntd = [nc.dram_tensor(f"cntd{f}", [P, GW], F32).ap() for f in range(2)]

    with ExitStack() as ctx:
        def sb(name, shape, dt=F32):
            return ctx.enter_context(nc.sbuf_tensor(name, shape, dt))

        def sem(name):
            return ctx.enter_context(nc.semaphore(name))

        ps = ctx.enter_context(nc.psum_tensor("ps", [P, 8, GW], F32))
        xs = sb("xs", [P, NT, D])
        xT = sb("xT", [P, NTOK])
        tb = sb("tb", [P, NT, TW])
        tbf = tb[:, :, :].rearrange("p a b -> p (a b)")
        ident = sb("ident", [P, P])
        ones = sb("ones", [P, P])
        bst = sb("bst", [P, NT, 6])
        sd = sb("sd", [P, 8, NT])
        s_mean, s_w, s_vp, s_rt, s_r, s_q, s_d = (sd[:, i, :] for i in range(7))
        stage = sb("stage", [P, 2 * TPG, D])
        waT = sb("waT", [P, 4, INNER])
        VV = sb("VV", [INNER, 4, INNER])
        RT = sb("RT", [P, P])
        Rm = sb("Rm", [P, P])
        XX = sb("XX", [P, 2, P])
        Zm = sb("Zm", [P, P])
        aI = sb("aI", [P, 2, P])
        BD = sb("BD", [P, 3, P])
        nrm = sb("nrm", [P, 4])
        arena = sb("arena", [P, 18440])
        off = [0]

        def carve(n):
            off[0] += n
            return arena[:, off[0] - n:off[0]]
        av = carve(2 * LT).rearrange("p (c t) -> p c t", c=2)
        lev = carve(2 * LT).rearrange("p (c t) -> p c t", c=2)
        SS = carve(2 * LT).rearrange("p (c t) -> p c t", c=2)
        XC = carve(2 * (LT + 1)).rearrange("p (c t) -> p c t", c=2)
        sq = carve(4 * GW).rearrange("p (c t) -> p c t", c=4)
        assert off[0] <= 18440
        mag = tbf[:, 0:2 * GW].rearrange("p (c t) -> p c t", c=2)
        rt2 = tbf[:, 2 * GW:4 * GW].rearrange("p (c t) -> p c t", c=2)
        rec = tbf[:, 4 * GW:5 * GW]
        MB = tbf[:, 3600:3600 + 3 * 2 * D].rearrange("p (i b d) -> p i b d", i=3, b=NB)
        T1 = sq[:, 0:2, :]
        T2 = sq[:, 2:4, :]

        f1w = sb("f1w", [P, NE, NF])
        f2w = sb("f2w", [P, NE, FT, D])
        b1 = sb("b1", [P, NE, FT])
        nwc = sb("nwc", [P, 1])
        rwp = sb("rwp", [P, 2, 32])
        rbc = sb("rbc", [P, 1])
        big = sb("big", [P, P], BF16)
        cf = sb("cf", [P, 2], F16)
        same = sb("same", [P, P], F16)
        before = sb("before", [P, P], F16)
        differ = sb("differ", [P, P], F16)
        srow = sb("srow", [P, CAP], F16)
        scol = sb("scol", [P, 2])
        bits = sb("bits", [P, 48], U32)
        nb = sb("nb", [P, 48], U32)
        pb = sb("pb", [P, 48], U32)
        ione = sb("ione", [P, 32], U32)
        ish = sb("ish", [P, 32], U32)
        tk = sb("tk", [P, 16])
        tku = tk[:, :].bitcast(U32)
        cn = sb("cn", [P, 4], F16)
        idx = sb("idx", [P, 2 * NE], U32)
        zero = tbf[:, 3000:3000 + TPG * AW]
        off[0] = 0
        L = carve(GW)
        cnt = carve(GW)
        csg = carve(GW)
        exs = carve(GW)
        lesum = carve(2 * NE)
        rinv = carve(NT)
        smx = carve(NT)
        gt, eq = (carve(GW // 2).bitcast(F16) for _ in range(2))
        cs16, cd16 = (carve(GW // 2).bitcast(F16) for _ in range(2))
        acc1 = arena[:, off[0]:off[0] + NT * AW].rearrange("p (t w) -> p t w", w=AW)
        G16 = carve(NE * CAP // 2).bitcast(F16).rearrange("p (e s) -> p e s", e=NE)
        RX = 8
        XE = carve(RX * 2 * TW).rearrange("p (r h w) -> p r h w", r=RX, h=2)
        xeT = carve(2 * CAP).rearrange("p (r s) -> p r s", r=2)
        hT = carve(2 * FT * CAP).rearrange("p (r f s) -> p r f s", r=2, f=FT)
        yv = carve(2 * 2 * AW).rearrange("p (r h w) -> p r h w", r=2, h=2)
        b2 = carve(NE * D).rearrange("p (e d) -> p e d", e=NE)
        assert off[0] <= 18440

        HD = 8
        NH = D // HD
        wqkv = sb("wqkv", [P, 3, P])
        wou = sb("wou", [P, D])
        sel = sb("sel", [P, 2, 32])
        off[0] = 0
        qn, kn, Zs, Zc, On = (carve(2 * GW).rearrange("p (r t) -> p r t", r=2) for _ in range(5))
        KV = carve(3 * GW).rearrange("p (r t) -> p r t", r=3)
        ST = carve(2 * HD * GW).rearrange("p (r i t) -> p r i t", r=2, i=HD)
        exq, exk = carve(GW), carve(GW)
        rden = carve(TPG * NH)
        rd = carve(2 * GW).rearrange("p (r t e h) -> p r t e h", r=2, t=TPG, h=NH)
        WV = carve(HD * P).rearrange("p (i h a) -> p i h a", i=HD, h=NH)
        assert off[0] <= 18440
        RS = tbf[:, HD * GW:(HD + 1) * GW]
        QS = tbf[:, 0:HD * GW].rearrange("p (i t) -> p i t", i=HD)
        wb_in = sem("wb_in")
        q_prod, q_neg, q_exp, q_ready = (sem(n) for n in ("q_prod", "q_neg", "q_exp", "q_ready"))
        k_prod, k_neg, k_exp, k_ready = (sem(n) for n in ("k_prod", "k_neg", "k_exp", "k_ready"))
        v_prod, v_used, state_ready, z_ready = (sem(n) for n in ("v_prod", "v_used", "state_ready", "z_ready"))
        qz_ready, qs_ready, den_prod, rden_ready = (sem(n) for n in ("qz_ready", "qs_ready", "den_prod", "rden_ready"))
        wv_ready, rd_ready, rs_ready, rep_prod, num_prod, on_ready = (sem(n) for n in ("wv_ready", "rd_ready", "rs_ready", "rep_prod", "num_prod", "on_ready"))
        fin_prod, x3_ready, shift_ready = sem("fin_prod"), sem("x3_ready"), sem("shift_ready")

        wf_in = [sem(f"wf_in{q}") for q in range(4)]
        router_in, b2_in, fb_in = sem("router_in"), sem("b2_in"), sem("fb_in")
        zeroed, tab_stored, cnt_stored, seg_in = sem("zeroed"), sem("tab_stored"), sem("cnt_stored"), sem("seg_in")
        xe_in = [sem(f"xe_in{r}") for r in range(RX)]
        scattered = [sem(f"scattered{i}") for i in range(2)]
        acc_in = [sem(f"acc_in{g}") for g in range(NG)]
        logit_prod, logit_T, logit_ready, exp_in, exped, tab_ready = (sem(n) for n in ("logit_prod", "logit_T", "logit_ready", "exp_in", "exped", "tab_ready"))
        counted, totalled, both_ready = sem("counted"), sem("totalled"), sem("both_ready")
        cand_ready, cnt_ready, seg16, seg_diff, onehot, slots_ready, idx_ready = (
            sem(n) for n in ("cand_ready", "cnt_ready", "seg16", "seg_diff", "onehot", "slots_ready", "idx_ready"))
        xe_T, xeT_ready, h_prod, h_ready, y_prod, y_ready, x_ready = (
            sem(n) for n in ("xe_T", "xeT_ready", "h_prod", "h_ready", "y_prod", "y_ready", "x_ready"))
        NR = 32
        BITS = 10
        NCOUNT = NR + 2

        x_in = [sem(f"x_in{g}") for g in range(NG)]
        wab_in, inv_in, wo_in, h0_in = sem("wab_in"), sem("inv_in"), sem("wo_in"), sem("h0_in")
        w_in = sem("w_in")
        stored = sem("stored")
        consts = sem("consts")
        dstep, pstep, gstep = sem("dstep"), sem("pstep"), sem("gstep")
        vp_ready, root_ready = sem("vp_ready"), sem("root_ready")
        normed, transposed, xT_ready = sem("normed"), sem("transposed"), sem("xT_ready")
        nw_sq, nw_norm, nw_Y, nw_Z, nw_X, nw_new = (sem(s) for s in ("nw_sq", "nw_norm", "nw_Y", "nw_Z", "nw_X", "nw_new"))
        bd_ready, mt_prod, mt_ready = sem("bd_ready"), sem("mt_prod"), sem("mt_ready")
        projected, squared, mag_ready, rooted, proj_used = (sem(s) for s in ("projected", "squared", "mag_ready", "rooted", "proj_used"))
        u_ready, u_used, s_ready = sem("u_ready"), sem("u_used"), sem("s_ready")
        lev_ready, raw_ready = sem("lev_ready"), sem("raw_ready")
        ao_ready, x1_ready = sem("ao_ready"), sem("x1_ready")

        N_WIDE, N_LAST = 18, 6
        HALVES = 2 * (N_WIDE + N_LAST)
        AT_NORM, AT_STEP, AT_COEF = 12, 6, 18
        WA, WB = 3.5, 3.5 * 3.5 / 4

        block = ctx.enter_context(nc.Block())

        @block.sync
        def _(sp):
            for t, src in ((RT[0:64, 0:64], vrT), (RT[64:128, 64:128], vrT), (RT[0:64, 64:128], viT), (RT[64:128, 0:64], viT),
                           (Rm[0:64, 0:64], vr), (Rm[64:128, 64:128], vr), (Rm[0:64, 64:128], vi), (Rm[64:128, 0:64], vi)):
                sp.dma_start(t, src).then_inc(inv_in, 16)
            for g in [b * NK + k for k in range(NK) for b in range(NB)]:
                b, k = divmod(g, NK)
                sp.dma_start(xs[:, g * TPG:(g + 1) * TPG, :],
                             x[b, k * GW:(k + 1) * GW, :].rearrange("(t p) d -> p t d", p=P)).then_inc(x_in[g], 16)
            sp.dma_start(waT[:, 0:2, :], wa).then_inc(wab_in, 16)
            sp.dma_start(waT[:, 2:4, :], wx).then_inc(wab_in, 16)
            for b in range(NB):
                sp.dma_start(XC[64 * b:64 * b + 64, 0, 0:1], h0r).then_inc(h0_in, 16)
                sp.dma_start(XC[64 * b:64 * b + 64, 1, 0:1], h0i).then_inc(h0_in, 16)
            for i in range(4):
                sp.dma_start(VV[:, i, :], vr if i < 2 else vi).then_inc(wo_in, 16)
            sp.wait_ge(consts, 2)
            for b in range(NB):
                sp.dma_start(MB[64 * b:64 * b + 64, 2, b, :], wo).then_inc(wo_in, 16)
            sp.dma_start(nwc[:, :], nw).then_inc(fb_in, 16)
            sp.dma_start(b1[:, :, :], f1b).then_inc(fb_in, 16)
            for c in range(NCH):
                sp.dma_start(rbc[c * NE:(c + 1) * NE, :], rb).then_inc(fb_in, 16)
            sp.dma_start(wqkv[:, :, :], wqkvT.rearrange("d (i n) -> d i n", i=3)).then_inc(wb_in, 16)
            sp.dma_start(wou[:, :], woutT).then_inc(wb_in, 16)
            sp.wait_ge(consts, 2)
            for i in range(2):
                sp.dma_start(rwp[:, i, i * NE:(i + 1) * NE], rwT).then_inc(router_in, 16)
            for q in range(4):
                e = slice(4 * q, 4 * q + 4)
                sp.dma_start(f1w[:, e, :], f1T[:, e, :]).then_inc(wf_in[q], 16)
                sp.dma_start(f2w[:, e, :, :], f2T[:, e, :, :]).then_inc(wf_in[q], 16)
            for f in range(2):
                for g in range(NG):
                    for i in range(2):
                        sp.dma_start(acc[f][i][g * GW:(g + 1) * GW, :].rearrange("(p r) w -> p (r w)", r=TPG), zero
                                     ).then_inc(zeroed, 16)

            def feed(f):
                sp.wait_ge(x1_ready if f == 0 else x3_ready, NG)
                sp.dma_start(b2[:, :, :], f2b.partition_broadcast(P)).then_inc(b2_in, 16)
                sp.wait_ge(tab_ready, f + 1)
                for q in range(4):
                    t = slice(8 * q, 8 * q + 8)
                    sp.dma_start(tab[f][q * 1024:(q + 1) * 1024, :].rearrange("(t p) w -> p t w", p=P), tb[:, t, :]
                                 ).then_inc(tab_stored, 16)
                sp.wait_ge(cnt_ready, f + 1)
                sp.dma_start(cntd[f][:, :], cnt).then_inc(cnt_stored, 16)
                sp.wait_ge(cnt_stored, 16 * (f + 1))
                for c in range(NCH):
                    sp.dma_start(csg[c * NE:(c + 1) * NE, :].rearrange("q (e t) -> q e t", e=NE),
                                 cntd[f][c * NE:(c + 1) * NE, :].rearrange("e (q t) -> q e t", q=NE)).then_inc(seg_in, 16)
                for i in range(2):
                    sp.wait_ge(scattered[i], 32 * NE // 2 * (f + 1))
                for g in range(NG):
                    for i, to in enumerate((tb[:, g * TPG:(g + 1) * TPG, 0:AW], acc1[:, g * TPG:(g + 1) * TPG, :])):
                        sp.dma_start(to, acc[f][i][g * GW:(g + 1) * GW, :].rearrange("(t p) w -> p t w", p=P)
                                     ).then_inc(acc_in[g], 16)

            feed(0)
            feed(1)
            for g in range(NG):
                b, k = divmod(g, NK)
                sp.wait_ge(x_ready, NG + g + 1)
                sp.dma_start(out[b, k * GW:(k + 1) * GW, :].rearrange("(t p) d -> p t d", p=P),
                             xs[:, g * TPG:(g + 1) * TPG, :]).then_inc(stored, 16)
            sp.wait_ge(stored, 16 * NG)

        @block.gpsimd
        def _(pool):
            G = Count(pool, gstep)
            G.did(pool.memset(ident[:, :], 0.0))
            G.did(pool.memset(ones[:, :], 1.0))
            G.settle()
            for t, fill in ((ident[:, :], 1.0),):
                pool.affine_select(out=t, in_=t, compare_op=ALU.not_equal, fill=fill, base=0,
                                   pattern=[[-1, P]], channel_multiplier=1).then_inc(consts, 1)
            pool.memset(zero, 0.0)
            pool.memset(MB, 0.0)
            pool.memset(rwp[:, :, :], 0.0).then_inc(consts, 1)
            pool.wait_ge(consts, 2)
            G.did(pool.memset(same[:, :], 0.0))
            G.did(pool.memset(ione[:, 0:31], 1))
            G.did(pool.memset(ione[:, 31:32], 0))
            G.did(pool.memset(ish[:, 31:32], 0))
            G.did(pool.iota(ish[:, 0:31].bitcast(I32), [[-1, 31]], base=30, channel_multiplier=0))
            G.did(pool.iota(srow[:, :], [[1, CAP]], base=0, channel_multiplier=0, allow_small_or_imprecise_dtypes=True))
            G.step(pool.iota(scol[:, :], [[P, 2]], base=0, channel_multiplier=1, allow_small_or_imprecise_dtypes=True))
            for d in range(-(NCH - 1), NCH):
                G.step(pool.affine_select(out=same[:, :], in_=same[:, :], compare_op=ALU.not_equal, fill=1.0, base=-NE * d,
                                          pattern=[[-1, P]], channel_multiplier=1))
            G.did(pool.tensor_scalar(big[:, :], same[:, :], 2.0 ** 114, None, ALU.mult))
            G.did(pool.memset(cf[:, 1:2], -(CAP - 0.5) / NCH))
            G.did(pool.affine_select(out=before[:, :], in_=same[:, :], compare_op=ALU.is_gt, fill=0.0, base=0,
                                     pattern=[[1, P]], channel_multiplier=-1))
            G.step(pool.tensor_copy(differ[:, :], ident[:, :]))
            pool.affine_select(out=differ[:, :], in_=differ[:, :], compare_op=ALU.not_equal, fill=-1.0, base=-1,
                               pattern=[[-1, P]], channel_multiplier=1).then_inc(consts, 1)
            G.step(pool.memset(sel[:, :, :], 0.0))
            for i in range(2):
                half = sel[:, i, i * NH:(i + 1) * NH]
                G.step(pool.affine_select(out=half, in_=ones[:, 0:NH], compare_op=ALU.is_ge, fill=0.0, base=0,
                                          pattern=[[-HD, NH]], channel_multiplier=1))
                G.did(pool.affine_select(out=half, in_=half, compare_op=ALU.is_ge, fill=0.0, base=HD - 1,
                                         pattern=[[HD, NH]], channel_multiplier=-1))
            G.settle()
            pool.tensor_copy(tk[:, 12:14], ones[:, 0:2]).then_inc(consts, 1)
            pool.wait_ge(proj_used, NK)
            pool.wait_ge(projected, NK)
            lo = 0
            A = av
            for lv in range(1, LEVELS):
                n = LT >> lv
                B = lev[:, :, lo:lo + n]
                lo += n
                t1 = xT[:, 0:2 * n].rearrange("p (c t) -> p c t", c=2)
                t2 = xT[:, 2 * n:4 * n].rearrange("p (c t) -> p c t", c=2)
                even, odd = A[:, :, 0::2], A[:, :, 1::2]
                G.did(pool.tensor_tensor(t1, odd[:, 0:1, :].to_broadcast([P, 2, n]), even, ALU.mult))
                G.step(pool.tensor_tensor(t2, odd[:, 1:2, :].to_broadcast([P, 2, n]), even, ALU.mult))
                pool.tensor_tensor(B[:, 0, :], t1[:, 0, :], t2[:, 1, :], ALU.subtract).then_inc(lev_ready, 1)
                pool.tensor_tensor(B[:, 1, :], t1[:, 1, :], t2[:, 0, :], ALU.add).then_inc(lev_ready, 1)
                pool.wait_ge(lev_ready, 2 * lv)
                A = B

            def feed(f):
                pool.wait_ge(tab_stored, 16 * 4 * (f + 1))
                pool.wait_ge(zeroed, 16 * NG * 4)

                def gather(e):
                    if e == 0:
                        pool.wait_ge(idx_ready, f + 1)
                    if e >= RX:
                        pool.wait_ge(y_ready, f * NE + e - RX + 1)
                    for h in range(2):
                        i = h * NE + e
                        pool.indirect_dma_start(out=XE[:, e % RX, h, :], out_offset=None, in_=tab[f],
                                                in_offset=bass.IndirectOffsetOnAxis(ap=idx[:, i:i + 1], axis=0)
                                                ).then_inc(xe_in[e % RX], 16)

                for e in range(RX - 1):
                    gather(e)
                for e in range(NE):
                    if e + RX - 1 < NE:
                        gather(e + RX - 1)
                    pool.wait_ge(y_ready, f * NE + e + 1)
                    if f * NE + e >= 2:
                        pool.wait_ge(scattered[e % 2], 32 * ((f * NE + e) // 2))
                    for h in range(2):
                        i = h * NE + e
                        pool.indirect_dma_start(out=acc[f][e % 2], out_offset=bass.IndirectOffsetOnAxis(ap=idx[:, i:i + 1], axis=0),
                                                in_=yv[:, e % 2, h, :], in_offset=None, compute_op=ALU.add
                                                ).then_inc(scattered[e % 2], 16)

            feed(0)
            for n in range(NG):
                r = n % 2
                pool.wait_ge(z_ready, n + 1)
                if n >= 2:
                    pool.wait_ge(den_prod, n - 1)
                pool.tensor_tensor(Zc[:, r, :], Zs[:, r, :], qn[:, r, :], ALU.mult).then_inc(qz_ready, 1)
                for i in range(HD):
                    u = n * HD + i
                    pool.wait_ge(state_ready, u + 1)
                    if n >= 1:
                        pool.wait_ge(num_prod, 2 * (n - 1) + i // 4 + 1)
                    pool.tensor_tensor(QS[:, i, :], ST[:, r, i, :], qn[:, r, :], ALU.mult).then_inc(qs_ready, 1)
            feed(1)

        @block.scalar
        def _(act):
            act.wait_ge(inv_in, 16 * 8)
            nc.scalar.activation(Zm[:, :], Rm[:, :], ACT.Square, accum_out=nrm[:, 0:1]).then_inc(nw_sq, 1)

            def root(run):
                act.wait_ge(vp_ready, run + 1)
                nc.scalar.activation(s_rt, s_vp, ACT.Sqrt).then_inc(root_ready, 1)

            def keep_xT(run, n, g):
                act.wait_ge(transposed, run * NG + n + 1)
                nc.scalar.activation(xT[:, g * GW:(g + 1) * GW], ps[:, 6 + n % 2, :], ACT.Copy).then_inc(xT_ready, 1)

            root(0)

            def squares(k):
                act.wait_ge(projected, k + 1)
                if k >= 1:
                    act.wait_ge(mag_ready, k)
                for q in range(4):
                    last = nc.scalar.activation(sq[:, q, :], ps[:, q, :], ACT.Square)
                last.then_inc(squared, 1)
                nc.scalar.activation(av[:, :, k * GW:(k + 1) * GW], ps[:, 0:2, :], ACT.Copy)
                nc.scalar.activation(XC[:, :, 1 + k * GW:1 + (k + 1) * GW], ps[:, 2:4, :], ACT.Copy).then_inc(raw_ready, 1)
                act.wait_ge(mag_ready, k + 1)
                if k >= 1:
                    act.wait_ge(proj_used, k)
                nc.scalar.activation(rt2, mag, ACT.Sqrt).then_inc(rooted, 1)

            for k in range(NK):
                if k >= 1:
                    squares(k - 1)
                for b in range(NB):
                    keep_xT(0, 2 * k + b, b * NK + k)
            squares(NK - 1)

            def feed(f):
                run = 1 + 2 * f
                root(run)
                act.wait_ge(fb_in, 16 * (2 + NCH))
                for n in range(NG):
                    act.wait_ge(transposed, run * NG + n + 1)
                    nc.scalar.activation(xT[:, n * GW:(n + 1) * GW], ps[:, 6 + n % 2, :], ACT.Copy, scale=nwc[:, 0:1]
                                         ).then_inc(xT_ready, 1)
                act.wait_ge(exp_in, f + 1)
                nc.scalar.activation(exs, exs, ACT.Exp).then_inc(exped, 1)
                for e in range(NE):
                    n = f * NE + e
                    act.wait_ge(h_prod, n + 1)
                    if n >= 2:
                        act.wait_ge(y_prod, n - 1)
                    for t in range(FT):
                        last = nc.scalar.activation(hT[:, e % 2, t, :],
                                                    ps[:, 2 * (e % 2) + t // 2, (t % 2) * CAP:(t % 2 + 1) * CAP],
                                                    ACT.Gelu, bias=b1[:, e, t:t + 1])
                    last.then_inc(h_ready, 1)

            feed(0)
            root(2)
            def norm(n):
                if n >= 2:
                    act.wait_ge(transposed, 2 * NG + n - 1)
                for t in range(TPG):
                    j = n * TPG + t
                    last = nc.scalar.activation(stage[:, (n % 2) * TPG + t, :], xs[:, j, :], ACT.Identity,
                                                scale=s_r[:, j:j + 1], bias=s_d[:, j:j + 1])
                last.then_inc(normed, 1)

            act.wait_ge(shift_ready, 1)
            norm(0)
            norm(1)
            act.wait_ge(x_ready, NG)
            act.wait_ge(wb_in, 32)
            for i in range(2):
                w = wqkv[:, 2, i::2].rearrange("p (h j) -> p j h", h=NH)
                for j in range(HD // 2):
                    last = nc.scalar.activation(WV[:, 4 * i + j, :, :], w[:, j, :].rearrange("p (h a) -> p h a", a=1
                                                                                            ).to_broadcast([P, NH, HD]), ACT.Copy)
            last.then_inc(wv_ready, 1)

            def exp_min(prod, bank, ex, ready, neg, exped, n):
                act.wait_ge(prod, n + 1)
                if n >= 1:
                    act.wait_ge(ready, n)
                nc.scalar.activation(ex, ps[:, bank, :], ACT.Relu, scale=-1.0).then_inc(neg, 1)
                act.wait_ge(neg, n + 1)
                nc.scalar.activation(ex, ex, ACT.Exp, scale=-1.0).then_inc(exped, 1)

            def spread(n):
                act.wait_ge(rden_ready, n + 1)
                if n >= 2:
                    act.wait_ge(rep_prod, n - 1)
                nc.scalar.activation(rd[:, n % 2, :, :, :],
                                     rden.rearrange("p (t a h) -> p t a h", t=TPG, a=1).to_broadcast([P, TPG, HD, NH]), ACT.Copy
                                     ).then_inc(rd_ready, 1)

            def keep_spread(n):
                act.wait_ge(rep_prod, n + 1)
                if n >= 1:
                    act.wait_ge(on_ready, n)
                nc.scalar.activation(RS, ps[:, 7, :], ACT.Copy).then_inc(rs_ready, 1)

            for n in range(NG):
                act.wait_ge(transposed, 2 * NG + n + 1)
                nc.scalar.activation(xT[:, n * GW:(n + 1) * GW], ps[:, 5, :], ACT.Copy).then_inc(xT_ready, 1)
                exp_min(q_prod, 6, exq, q_ready, q_neg, q_exp, n)
                exp_min(k_prod, 5, exk, k_ready, k_neg, k_exp, n)
                if n + 2 < NG:
                    norm(n + 2)
                if n >= 2:
                    keep_spread(n - 2)
                if n >= 1:
                    spread(n - 1)
            keep_spread(NG - 2)
            spread(NG - 1)
            keep_spread(NG - 1)
            feed(1)

        @block.tensor
        def _(pe):
            pe.wait_ge(consts, 1)

            def transposes(run, n, tiles):
                pe.wait_ge(normed, run * NG + n + 1)
                if run * NG + n >= 2:
                    pe.wait_ge(xT_ready, run * NG + n - 1)
                for t in range(TPG):
                    last = nc.tensor.transpose(ps[:, 6 + n % 2, t * P:(t + 1) * P], tiles(t), ident[:, :])
                last.then_inc(transposed, 1)

            pe.wait_ge(nw_sq, 1)
            nc.tensor.matmul(ps[:, 5, 0:1], ones[:, :], nrm[:, 0:1], start=True, stop=True).then_inc(nw_norm, 1)
            done = [0]

            def inverse(upto):
                while done[0] < min(upto, HALVES):
                    i, half = divmod(done[0], 2)
                    if half == 0:
                        pe.wait_ge(nw_new, i + 1)
                        nc.tensor.matmul(ps[:, 5, 0:P], RT[:, :], XX[:, 0, :], start=True, stop=True).then_inc(nw_Y, 1)
                    else:
                        pe.wait_ge(nw_Z, i + 1)
                        nc.tensor.matmul(ps[:, 4, 0:P], XX[:, 1, :], Zm[:, :], start=True, stop=True)
                        nc.tensor.matmul(ps[:, 4, P:2 * P], Zm[:, :], XX[:, 1, :], start=True, stop=True).then_inc(nw_X, 1)
                    done[0] += 1

            for k in range(NK):
                for b in range(NB):
                    inverse(AT_NORM + 2 + AT_STEP * k + b)
                    if k == 0 and b == 0:
                        pe.wait_ge(wab_in, 32)
                    transposes(0, 2 * k + b, lambda t: stage[:, b * TPG + t, :])
                for b in range(NB):
                    pe.wait_ge(xT_ready, 2 * k + b + 1)
                if k >= 1:
                    pe.wait_ge(raw_ready, k)
                for q in range(4):
                    if q == 2:
                        inverse(AT_NORM + 4 + AT_STEP * k)
                    for b in range(NB):
                        last = nc.tensor.matmul(ps[64 * b:64 * b + 64, q, :], waT[:, q, :],
                                                xT[:, (b * NK + k) * GW:(b * NK + k + 1) * GW], start=True, stop=True)
                last.then_inc(projected, 1)
            inverse(HALVES)
            pe.wait_ge(wo_in, 16 * (2 + 4))
            pe.wait_ge(xT_ready, NG)
            nc.tensor.matmul(ps[:, 6, 0:D], VV[:, 0:2, :].rearrange("p a b -> p (a b)"), MB[0:64, 2, 0, :], start=True, stop=True)
            nc.tensor.matmul(ps[:, 6, D:2 * D], VV[:, 2:4, :].rearrange("p a b -> p (a b)"), MB[0:64, 2, 0, :],
                             start=True, stop=True).then_inc(mt_prod, 1)
            pe.wait_ge(bd_ready, 1)
            pe.wait_ge(h0_in, 16 * 4)
            pe.wait_ge(mt_ready, 1)
            for k in range(NK):
                bank = 4 + 2 * (k % 2)
                if k >= 2:
                    pe.wait_ge(u_used, k - 1)
                pe.wait_ge(proj_used, k + 1)
                xr, xi = XC[:, 0, k * GW:(k + 1) * GW], XC[:, 1, k * GW:(k + 1) * GW]
                nc.tensor.matmul(ps[:, bank, :], BD[:, 0, :], xr, start=True, stop=False)
                nc.tensor.matmul(ps[:, bank, :], BD[:, 2, :], xi, start=False, stop=True)
                nc.tensor.matmul(ps[:, bank + 1, :], BD[:, 1, :], xr, start=True, stop=False)
                nc.tensor.matmul(ps[:, bank + 1, :], BD[:, 0, :], xi, start=False, stop=True).then_inc(u_ready, 1)
            for n in range(2 * NK):
                pe.wait_ge(s_ready, 1 if n < NK else 2)
                if n >= 4:
                    pe.wait_ge(x1_ready, n - 3)
                for t in range(2):
                    at = (2 * n + t) * P
                    for i, lhs in enumerate((SS[:, 0, at:at + P], SS[:, 1, at:at + P], XC[:, 0, at + 1:at + 1 + P])):
                        last = nc.tensor.matmul(ps[:, n % 4, t * 2 * D:(t + 1) * 2 * D], lhs,
                                                MB[:, i, :, :].rearrange("p b d -> p (b d)"), start=(i == 0), stop=(i == 2))
                last.then_inc(ao_ready, 1)

            def feed(f):
                run = 1 + 2 * f
                for n in range(NG):
                    transposes(run, n, lambda t: tb[:, n * TPG + t, 0:D])
                pe.wait_ge(router_in, 32)
                pe.wait_ge(xT_ready, run * NG + NG)
                for i in range(2):
                    for c in range(4):
                        g = 2 * c + i
                        last = nc.tensor.matmul(ps[32 * c:32 * c + 32, 0, :], rwp[:, i, :], xT[:, g * GW:(g + 1) * GW],
                                                start=(i == 0), stop=(i == 1), skip_group_check=True)
                last.then_inc(logit_prod, 1)
                pe.wait_ge(logit_ready, f + 1)
                for q in range(TPG):
                    last = nc.tensor.transpose(ps[:, 1, q * P:(q + 1) * P], L[:, q * P:(q + 1) * P], ident[:, :])
                last.then_inc(logit_T, 1)
                def total(k):
                    if isinstance(k, int) and k == 0:
                        pe.wait_ge(counted, f * NCOUNT + 1)
                    else:
                        pe.wait_ge(cand_ready, k + f * NR)
                    nc.tensor.matmul(ps[:, 2, 0:1], big[:, :], cf[:, 1:2], start=True, stop=False)
                    pe.wait_ge(counted, k + (f * NCOUNT + 1))
                    nc.tensor.matmul(ps[:, 2, 0:1], big[:, :], cf[:, 0:1], start=False, stop=True).then_inc(totalled, 1)
                total(0)
                total(1)
                with pe.Fori(0, NR - 2, BITS) as r:
                    for j in range(BITS):
                        total(r + (j + 2))
                pe.wait_ge(counted, f * NCOUNT + NR + 1)
                nc.tensor.matmul(ps[:, 2, 1:2], same[:, :], cn[:, 1:2], start=True, stop=True)
                nc.tensor.matmul(ps[:, 2, 2:3], before[:, :], cn[:, 2:3], start=True, stop=True).then_inc(totalled, 1)
                pe.wait_ge(counted, f * NCOUNT + NR + 2)
                nc.tensor.matmul(ps[:, 2, 3:4], before[:, :], cn[:, 3:4], start=True, stop=True).then_inc(totalled, 1)
                pe.wait_ge(seg16, f + 1)
                nc.tensor.matmul(ps[:, 3, :], differ[:, :], cs16, start=True, stop=True).then_inc(seg_diff, 1)
                pe.wait_ge(onehot, f + 1)
                for h in range(2):
                    for e in range(NE):
                        last = nc.tensor.matmul(ps[:, 4 + h, e * 32:e * 32 + 32], G16[:, e, h * P:(h + 1) * P],
                                                cd16[:, e * 32:e * 32 + 32], start=True, stop=True)
                last.then_inc(slots_ready, 1)
                pe.wait_ge(idx_ready, f + 1)

                def turn(e):
                    n = f * NE + e
                    pe.wait_ge(xe_in[e % RX], 32 * (f * NE // RX + e // RX + 1))
                    if n >= 2:
                        pe.wait_ge(xeT_ready, n - 1)
                    for h in range(2):
                        last = nc.tensor.transpose(ps[:, 4 + e % 2, h * P:(h + 1) * P],
                                                   XE[:, e % RX, h, 0:D], ident[:, :])
                    last.then_inc(xe_T, 1)

                turn(0)
                for e in range(NE + 1):
                    n = f * NE + e
                    if e + 1 < NE:
                        turn(e + 1)
                    if e < NE:
                        if e % 4 == 0:
                            pe.wait_ge(wf_in[e // 4], 32)
                        pe.wait_ge(xeT_ready, n + 1)
                        if n >= 2:
                            pe.wait_ge(h_ready, n - 1)
                        for t in range(FT):
                            last = nc.tensor.matmul(ps[:, 2 * (e % 2) + t // 2, (t % 2) * CAP:(t % 2 + 1) * CAP],
                                                    f1w[:, e, t * P:(t + 1) * P], xeT[:, e % 2, :], start=True, stop=True)
                        last.then_inc(h_prod, 1)
                    if e >= 1:
                        m = e - 1
                        pe.wait_ge(h_ready, n)
                        if n - 1 >= 2:
                            pe.wait_ge(y_ready, n - 2)
                        for h in range(2):
                            for t in range(FT):
                                last = nc.tensor.matmul(ps[:, 6 + m % 2, h * P:(h + 1) * P], hT[:, m % 2, t, h * P:(h + 1) * P],
                                                        f2w[:, m, t, :], start=(t == 0), stop=(t == FT - 1))
                        last.then_inc(y_prod, 1)

            feed(0)

            def to_xT(m):
                pe.wait_ge(normed, 2 * NG + m + 1)
                pe.wait_ge(x_ready, NG)
                if m >= 1:
                    pe.wait_ge(k_ready, m)
                for t in range(TPG):
                    last = nc.tensor.transpose(ps[:, 5, t * P:(t + 1) * P], stage[:, (m % 2) * TPG + t, :], ident[:, :])
                last.then_inc(transposed, 1)

            def project_q(m):
                pe.wait_ge(xT_ready, 2 * NG + m + 1)
                if m >= 1:
                    pe.wait_ge(q_ready, m)
                if m >= 2:
                    pe.wait_ge(rden_ready, m - 1)
                nc.tensor.matmul(ps[:, 6, :], wqkv[:, 0, :], xT[:, m * GW:(m + 1) * GW], start=True, stop=True).then_inc(q_prod, 1)

            def project_k(m):
                nc.tensor.matmul(ps[:, 5, :], wqkv[:, 1, :], xT[:, m * GW:(m + 1) * GW], start=True, stop=True).then_inc(k_prod, 1)

            def spread_v(n, i):
                u = n * HD + i
                if u >= 4:
                    pe.wait_ge(v_used, u - 3)
                pe.wait_ge(xT_ready, 2 * NG + n + 1)
                if u == 0:
                    pe.wait_ge(wv_ready, 1)
                nc.tensor.matmul(ps[:, u % 4, :], WV[:, i, :, :].rearrange("p h a -> p (h a)"), xT[:, n * GW:(n + 1) * GW], start=True, stop=True).then_inc(v_prod, 1)

            def numerator(n, i):
                pe.wait_ge(qs_ready, n * HD + 4 * i + 4)
                if i == 0 and n >= 1:
                    pe.wait_ge(on_ready, n)
                for j in range(4):
                    last = nc.tensor.matmul(ps[32 * j:32 * j + 32, 4, :], sel[:, i, :], QS[:, 4 * i + j, :],
                                            start=(i == 0), stop=(i == 1), skip_group_check=True)
                last.then_inc(num_prod, 1)

            def denominator(n):
                pe.wait_ge(qz_ready, n + 1)
                if n + 1 < NG:
                    pe.wait_ge(q_ready, n + 2)
                for t in range(TPG):
                    last = nc.tensor.matmul(ps[:, 6, t * NH:(t + 1) * NH], Zc[:, n % 2, t * P:(t + 1) * P], sel[:, 0, 0:NH],
                                            start=True, stop=True)
                last.then_inc(den_prod, 1)

            def spread_reciprocals(n):
                pe.wait_ge(rd_ready, n + 1)
                if n >= 1:
                    pe.wait_ge(x3_ready, n)
                for t in range(TPG):
                    last = nc.tensor.matmul(ps[:, 7, t * P:(t + 1) * P], rd[:, n % 2, t, :, :].rearrange("p e h -> p (e h)"), ident[:, :], start=True, stop=True)
                last.then_inc(rep_prod, 1)

            def project_out(n):
                pe.wait_ge(on_ready, n + 1)
                for t in range(TPG):
                    last = nc.tensor.matmul(ps[:, 7, t * P:(t + 1) * P], On[:, n % 2, t * P:(t + 1) * P], wou[:, :],
                                            start=True, stop=True)
                last.then_inc(fin_prod, 1)

            pe.wait_ge(consts, 4)
            pe.wait_ge(wb_in, 32)
            to_xT(0)
            project_q(0)
            project_k(0)
            for n in range(NG + 2):
                for i in range(HD):
                    if n < NG:
                        spread_v(n, i)
                    if i == 0 and 1 <= n <= NG:
                        numerator(n - 1, 0)
                    if i == 0 and n >= 2:
                        project_out(n - 2)
                    if n + 1 < NG and i in (1, 2, 3):
                        (to_xT, project_q, project_k)[i - 1](n + 1)
                    if i == 3 and 1 <= n <= NG:
                        numerator(n - 1, 1)
                    if i == 4 and 1 <= n <= NG:
                        spread_reciprocals(n - 1)
                    if i == 6 and n < NG:
                        denominator(n)
            feed(1)

        @block.vector
        def _(dve):
            V = Count(dve, dstep)

            def tt(o, a, b, op):
                return nc.vector.tensor_tensor(o, a, b, op)

            def ts(o, a, s1, s2, op0, op1=None, **kw):
                if op1 is None:
                    return nc.vector.tensor_scalar(o, a, s1, s2, op0, **kw)
                return nc.vector.tensor_scalar(o, a, s1, s2, op0, op1, **kw)

            def stt(o, a, s, b, op0, op1, **kw):
                return nc.vector.scalar_tensor_tensor(o, a, s, b, op0, op1, **kw)

            def stats(g):
                for t in range(TPG):
                    V.did(nc.vector.bn_stats(bst[:, g * TPG + t, :], xs[:, g * TPG + t, :]))

            def scales(run, mul, eps, between=lambda: None):
                V.settle()
                V.did(tt(s_d, bst[:, :, 1], bst[:, :, 4], ALU.subtract))
                V.did(tt(s_w, bst[:, :, 2], bst[:, :, 5], ALU.add))
                V.step(tt(s_mean, bst[:, :, 1], bst[:, :, 4], ALU.add))
                V.did(nc.vector.tensor_scalar(s_mean, s_mean, 0.5, None, ALU.mult))
                V.step(tt(s_d, s_d, s_d, ALU.mult))
                V.step(nc.vector.scalar_tensor_tensor(s_w, s_d, P / 4.0, s_w, ALU.mult, ALU.add))
                nc.vector.tensor_scalar(s_vp, s_w, mul / P, eps, ALU.mult, ALU.add).then_inc(vp_ready, 1)
                between()
                dve.wait_ge(root_ready, run + 1)
                V.step(nc.vector.reciprocal(s_r, s_rt))
                V.step(tt(s_q, s_r, s_r, ALU.mult))
                V.step(tt(s_q, s_q, s_vp, ALU.mult))
                V.step(nc.vector.tensor_scalar(s_q, s_q, -0.5, 1.5, ALU.mult, ALU.add))
                V.step(tt(s_r, s_r, s_q, ALU.mult))

            def normalise(run, n, g, dst):
                for t in range(TPG):
                    j = g * TPG + t
                    last = nc.vector.tensor_scalar(dst(t), xs[:, j, :], s_mean[:, j:j + 1], s_r[:, j:j + 1],
                                                   ALU.subtract, ALU.mult)
                last.then_inc(normed, 1)

            dve.wait_ge(inv_in, 16 * 8)
            dve.wait_ge(nw_sq, 1)
            dve.wait_ge(consts, 1)
            V.did(nc.vector.memset(BD[:, :, :], 0.0))
            V.did(nc.vector.tensor_scalar(Rm[0:64, 64:128], Rm[0:64, 64:128], -1.0, None, ALU.mult))
            V.did(nc.vector.tensor_scalar(RT[64:128, 0:64], RT[64:128, 0:64], -1.0, None, ALU.mult))
            V.did(nc.vector.tensor_scalar(aI[:, 0, :], ident[:, :], WA / WB, None, ALU.mult))
            V.did(nc.vector.tensor_scalar(aI[:, 1, :], ident[:, :], 2.0, None, ALU.mult))
            dve.wait_ge(nw_norm, 1)
            V.step(nc.vector.tensor_scalar(nrm[:, 1:2], ps[:, 5, 0:1], 0.5, None, ALU.mult))
            V.step(nc.vector.reciprocal(nrm[:, 2:3], nrm[:, 1:2]))
            nc.vector.tensor_scalar(XX[:, 0, :], RT[:, :], nrm[:, 2:3], None, ALU.mult)
            nc.vector.tensor_scalar(XX[:, 1, :], Rm[:, :], nrm[:, 2:3], None, ALU.mult).then_inc(nw_new, 1)
            done = [0]

            def inverse(n=1):
                for _ in range(n):
                    if done[0] == HALVES:
                        return
                    i, half = divmod(done[0], 2)
                    if half == 0:
                        dve.wait_ge(nw_Y, i + 1)
                        stt(Zm[:, :], ps[:, 5, 0:P], -1.0, aI[:, 0 if i < N_WIDE else 1, :], ALU.mult, ALU.add).then_inc(nw_Z, 1)
                    else:
                        dve.wait_ge(nw_X, i + 1)
                        ts(XX[:, :, :].rearrange("p a b -> p (a b)"), ps[:, 4, 0:2 * P], WB if i < N_WIDE else 1.0, None, ALU.mult
                           ).then_inc(nw_new, 1)
                    done[0] += 1

            order = [b * NK + k for k in range(NK) for b in range(NB)]
            for g in order:
                dve.wait_ge(x_in[g], 16)
                stats(g)
                inverse()
            scales(0, 1.0, EPS, lambda: inverse())
            inverse(AT_NORM - done[0])
            assert done[0] == AT_NORM

            def norm_a(k):
                for b in range(NB):
                    n = 2 * k + b
                    if n >= 2:
                        dve.wait_ge(transposed, n - 1)
                    normalise(0, n, b * NK + k, lambda t: stage[:, b * TPG + t, :])
                    inverse()

            def coefficients(k):
                assert done[0] >= min(HALVES, AT_NORM + 4 + AT_STEP * k), (done[0], k)
                dve.wait_ge(squared, k + 1)
                if k >= 1:
                    dve.wait_ge(rooted, k)
                nc.vector.tensor_tensor(mag, sq[:, 0:4:2, :], sq[:, 1:4:2, :], ALU.add).then_inc(mag_ready, 1)
                inverse()
                dve.wait_ge(mag_ready, k + 1)
                V.step(nc.vector.tensor_scalar(rec, mag[:, 0, :], 1.0, None, ALU.add))
                V.step(nc.vector.reciprocal(rec, rec))
                inverse()
                dve.wait_ge(rooted, k + 1)
                dve.wait_ge(raw_ready, k + 1)
                X = XC[:, :, 1 + k * GW:1 + (k + 1) * GW]
                V.did(tt(X, X, rt2[:, 1:2, :].to_broadcast([P, 2, GW]), ALU.mult))
                inverse()
                V.step(tt(rec, rec, rt2[:, 0, :], ALU.mult))
                A = av[:, :, k * GW:(k + 1) * GW]
                tt(A, A, rec.rearrange("p (a t) -> p a t", a=1).to_broadcast([P, 2, GW]), ALU.mult).then_inc(proj_used, 1)
                inverse()

            norm_a(0)
            for k in range(NK):
                if k + 1 < NK:
                    norm_a(k + 1)
                inverse(min(HALVES, AT_COEF + AT_STEP * k) - done[0])
                coefficients(k)
            inverse(HALVES)
            dve.wait_ge(nw_new, N_WIDE + N_LAST + 1)
            lo_, hi_ = slice(0, 64), slice(64, 128)
            V.did(nc.vector.tensor_copy(BD[lo_, 0, lo_], XX[lo_, 1, lo_]))
            V.did(nc.vector.tensor_copy(BD[hi_, 0, hi_], XX[hi_, 1, hi_]))
            V.did(nc.vector.tensor_copy(BD[lo_, 1, lo_], XX[lo_, 1, hi_]))
            V.did(nc.vector.tensor_scalar(BD[hi_, 1, hi_], XX[hi_, 1, lo_], -1.0, None, ALU.mult))
            V.did(nc.vector.tensor_scalar(BD[lo_, 2, lo_], XX[lo_, 1, hi_], -1.0, None, ALU.mult))
            nc.vector.tensor_copy(BD[hi_, 2, hi_], XX[hi_, 1, lo_]).then_inc(bd_ready, 1)
            dve.wait_ge(mt_prod, 1)
            for b, r in enumerate((lo_, hi_)):
                V.did(nc.vector.tensor_copy(MB[r, 0, b, :], ps[r, 6, 0:D]))
                last = nc.vector.tensor_scalar(MB[r, 1, b, :], ps[r, 6, D:2 * D], -1.0, None, ALU.mult)
            last.then_inc(mt_ready, 1)

            def times(cr, ci, n, q, o, add_to):
                t1, t2 = T1[:, :, 0:n], T2[:, :, 0:n]
                V.did(tt(t1, cr.to_broadcast([P, 2, n]), q, ALU.mult))
                V.step(tt(t2, ci.to_broadcast([P, 2, n]), q, ALU.mult))
                to = t1 if add_to else o
                if add_to:
                    V.did(tt(t1[:, 0, :], t1[:, 0, :], t2[:, 1, :], ALU.subtract))
                    V.step(tt(t1[:, 1, :], t1[:, 1, :], t2[:, 0, :], ALU.add))
                    V.step(tt(o, o, t1, ALU.add))
                else:
                    V.did(tt(to[:, 0, :], t1[:, 0, :], t2[:, 1, :], ALU.subtract))
                    V.step(tt(to[:, 1, :], t1[:, 1, :], t2[:, 0, :], ALU.add))

            for k in range(NK):
                H = GW // 2
                dve.wait_ge(u_ready, k + 1)
                dve.wait_ge(proj_used, k + 1)
                e, o = slice(k * GW, (k + 1) * GW, 2), slice(k * GW + 1, (k + 1) * GW, 2)
                U = ps[:, 4 + 2 * (k % 2):6 + 2 * (k % 2), :]
                times(av[:, 0:1, e], av[:, 1:2, e], H, U[:, :, 0::2], SS[:, :, e], False)
                v = mag[:, :, 0:H]
                tt(v, SS[:, :, e], U[:, :, 1::2], ALU.add).then_inc(u_used, 1)
                dve.wait_ge(u_used, k + 1)
                times(av[:, 0:1, o], av[:, 1:2, o], H, v, SS[:, :, o], False)
            lv_at = [0] * (LEVELS + 1)
            for lv in range(2, LEVELS):
                lv_at[lv] = lv_at[lv - 1] + (LT >> (lv - 1))
            for lv in range(1, LEVELS):
                s, n = 1 << lv, LT >> (lv + 1)
                dve.wait_ge(lev_ready, 2 * lv)
                A = lev[:, :, lv_at[lv]:lv_at[lv] + 2 * n]
                for c0 in range(0, n, GW):
                    w = min(GW, n - c0)
                    q = SS[:, :, s - 1 + c0 * 2 * s::2 * s][:, :, 0:w]
                    o = SS[:, :, 2 * s - 1 + c0 * 2 * s::2 * s][:, :, 0:w]
                    times(A[:, 0:1, 2 * c0 + 1::2][:, :, 0:w], A[:, 1:2, 2 * c0 + 1::2][:, :, 0:w], w, q, o, True)
            for lv in range(LEVELS - 2, -1, -1):
                s, n = 1 << lv, (LT >> (lv + 1)) - 1
                A = lev[:, :, lv_at[lv]:lv_at[lv] + 2 * (n + 1)] if lv else av
                for c0 in range(0, n, GW):
                    w = min(GW, n - c0)
                    q = SS[:, :, 2 * s - 1 + c0 * 2 * s::2 * s][:, :, 0:w]
                    o = SS[:, :, 3 * s - 1 + c0 * 2 * s::2 * s][:, :, 0:w]
                    times(A[:, 0:1, 2 * c0 + 2::2][:, :, 0:w], A[:, 1:2, 2 * c0 + 2::2][:, :, 0:w], w, q, o, True)
                    if lv == 0:
                        nc.vector.tensor_copy(nrm[:, 3:4], nrm[:, 2:3]).then_inc(s_ready, 1)
            for n in range(2 * NK):
                dve.wait_ge(ao_ready, n + 1)
                row = xs[:, :, :].rearrange("p (b j) d -> p b j d", b=NB)[:, :, 2 * n:2 * n + 2, :]
                tt(row, row, ps[:, n % 4, :].rearrange("p (t b d) -> p b t d", t=2, b=NB), ALU.add).then_inc(x1_ready, 1)
                dve.wait_ge(x1_ready, n + 1)
                for j in (2 * n, 2 * n + 1, NT // 2 + 2 * n, NT // 2 + 2 * n + 1):
                    V.did(nc.vector.bn_stats(bst[:, j, :], xs[:, j, :]))

            def feed(f):
                run = 1 + 2 * f
                scales(run, 1.0 + EPS, EPS * EPS)
                dve.wait_ge(zeroed, 16 * NG * 4)
                for g in range(NG):
                    normalise(run, g, g, lambda t: tb[:, g * TPG + t, 0:D])
                dve.wait_ge(logit_prod, f + 1)
                ts(L, ps[:, 0, :], rbc[:, 0:1], None, ALU.add).then_inc(logit_ready, 1)
                dve.wait_ge(logit_T, f + 1)
                lt = ps[:, 1, :].rearrange("p (t e) -> p t e", e=NE)
                ex = exs.rearrange("p (t e) -> p t e", e=NE)

                def over(v):
                    return v.rearrange("p (t e) -> p t e", e=1).to_broadcast([P, NT, NE])
                V.step(nc.vector.tensor_reduce(smx, lt, AX.X, ALU.max))
                tt(ex, lt, over(smx), ALU.subtract).then_inc(exp_in, 1)
                cand, neg, thr, lo, hi, hit, miss, pos = (tku[:, i:i + 1] for i in range(8))
                M = cand
                junk = gt
                base = f * NCOUNT
                dve.wait_ge(consts, 3)
                if f == 0:
                    V.step(tt(bits[:, 0:32], ione[:, :], ish[:, :], ALU.logical_shift_left))
                ts(junk, L, 0.0, None, ALU.is_ge, ALU.add, accum_out=cf[:, 0:1]).then_inc(counted, 1)
                dve.wait_ge(exped, f + 1)
                V.step(nc.vector.tensor_reduce(smx, ex, AX.X, ALU.add))
                V.step(nc.vector.reciprocal(smx, smx))
                for q in range(TPG):
                    prob = tt(tb[:, q::TPG, D:TW], ex[:, q * NCH:(q + 1) * NCH, :], over(smx)[:, q * NCH:(q + 1) * NCH, :], ALU.mult)
                prob.then_inc(tab_ready, 1)
                dve.wait_ge(totalled, base + 1)
                V.did(ts(pos, ps[:, 2, 0:1], 0.0, None, ALU.is_gt))
                V.step(ts(neg, ps[:, 2, 0:1], 0.0, None, ALU.is_lt))
                V.did(tt(pb[:, 0:32], bits[:, 0:32], pos.to_broadcast([P, 32]), ALU.mult))
                V.did(tt(nb[:, 0:32], bits[:, 0:32], neg.to_broadcast([P, 32]), ALU.mult))
                V.step(ts(cand, neg, 31, None, ALU.logical_shift_left))
                tt(cand, cand, bits[:, 0:1], ALU.bitwise_or).then_inc(cand_ready, 1)
                V.settle()
                dve.wait_ge(cand_ready, f * NR + 1)

                def bit(r):
                    ts(junk, L, cand.bitcast(F32), None, ALU.is_ge, ALU.add, accum_out=cf[:, 0:1]).then_inc(counted, 1)
                    stt(hit, cand, nb[:, bass.ds(r, 1)], bits[:, bass.ds(r + 1, 1)], ALU.bitwise_xor, ALU.bitwise_or
                        ).then_inc(both_ready, 1)
                    stt(miss, cand, pb[:, bass.ds(r, 1)], bits[:, bass.ds(r + 1, 1)], ALU.bitwise_xor, ALU.bitwise_or
                        ).then_inc(both_ready, 1)
                    dve.wait_ge(both_ready, r * 2 + (f * 2 * (NR - 1) + 2))
                    dve.wait_ge(totalled, r + (base + 2))
                    ts(cand.bitcast(F32), ps[:, 2, 0:1], miss.bitcast(F32), hit.bitcast(F32), ALU.max, ALU.min).then_inc(cand_ready, 1)
                    dve.wait_ge(cand_ready, r + (f * NR + 2))
                bit(0)
                with dve.Fori(0, NR - 2, BITS) as r:
                    for j in range(BITS):
                        bit(r + (j + 1))
                V.did(ts(lo, M, 0xFFFF, None, ALU.bitwise_and))
                V.step(ts(hi, M, 16, None, ALU.logical_shift_right))
                V.step(tt(lo, lo, neg, ALU.add))
                V.step(ts(cand, lo, 16, None, ALU.logical_shift_right))
                V.step(tt(hi, hi, cand, ALU.add))
                V.did(ts(lo, lo, 0xFFFF, None, ALU.bitwise_and))
                V.step(ts(hi, hi, 16, None, ALU.logical_shift_left))
                V.step(tt(thr, hi, lo, ALU.bitwise_or))
                T = thr.bitcast(F32)
                V.did(ts(gt, L, T, None, ALU.is_gt, ALU.add, accum_out=cn[:, 1:2]))
                ts(eq, L, T, None, ALU.is_equal, ALU.add, accum_out=cn[:, 2:3]).then_inc(counted, 1)
                dve.wait_ge(counted, base + NR + 1)
                V.did(nc.vector.tensor_tensor_scan(cnt, eq, eq, 0.0, ALU.add, ALU.max))
                dve.wait_ge(totalled, base + NR + 1)
                need = tk[:, 8:9]
                V.step(ts(need, ps[:, 2, 1:2], -1.0, float(CAP), ALU.mult, ALU.add))
                V.step(tt(need, need, ps[:, 2, 2:3], ALU.subtract))
                V.step(stt(eq, cnt, need, eq, ALU.is_le, ALU.mult))
                stt(gt, eq, 0.0, gt, ALU.add, ALU.add, accum_out=cn[:, 3:4]).then_inc(counted, 1)
                dve.wait_ge(counted, base + NR + 2)
                dve.wait_ge(totalled, base + NR + 2)
                V.step(nc.vector.tensor_copy(tk[:, 9:10], ps[:, 2, 3:4]))
                nc.vector.tensor_tensor_scan(cnt, gt, gt, tk[:, 9:10], ALU.add, ALU.max).then_inc(cnt_ready, 1)
                dve.wait_ge(seg_in, 16 * NCH * (f + 1))
                nc.vector.tensor_copy(cs16, csg).then_inc(seg16, 1)
                for e in range(NE):
                    V.did(ts(G16[:, e, :], srow[:, :], csg[:, 32 * e + 31:32 * e + 32], None, ALU.is_lt))
                dve.wait_ge(seg_diff, f + 1)
                V.step(nc.vector.tensor_copy(cd16, ps[:, 3, :]))
                nc.vector.memset(cd16.rearrange("p (e t) -> p e t", e=NE)[:, :, 31:32], 1.0).then_inc(onehot, 1)
                dve.wait_ge(slots_ready, f + 1)
                lev3 = G16.rearrange("p e s -> p (e s)")[:, 0:2 * NE * 31].rearrange("p (h t) -> p h t", h=2 * NE)
                for h in range(2):
                    V.did(ts(lev3[:, h * NE:(h + 1) * NE, :], ps[:, 4 + h, :].rearrange("p (e t) -> p e t", e=NE)[:, :, 0:31],
                             scol[:, h:h + 1], None, ALU.is_le))
                V.settle()
                V.step(nc.vector.tensor_reduce(lesum, lev3, AX.X, ALU.add))
                col = ps[:, 4:6, :].rearrange("p h (e t) -> p (h e) t", e=NE)[:, :, 31:32]
                V.step(stt(lesum, col.rearrange("p a t -> p (a t)"), -32.0, lesum, ALU.mult, ALU.add))
                ts(idx[:, :], lesum, 32.0 * P, None, ALU.add).then_inc(idx_ready, 1)
                dve.wait_ge(b2_in, 16 * (f + 1))

                def keep_xe(e):
                    n = f * NE + e
                    dve.wait_ge(xe_T, n + 1)
                    if n >= 2:
                        dve.wait_ge(h_prod, n - 1)
                    ts(xeT[:, e % 2, :], ps[:, 4 + e % 2, 0:CAP], nwc[:, 0:1], None, ALU.mult
                       ).then_inc(xeT_ready, 1)

                keep_xe(0)
                keep_xe(1)
                for e in range(NE):
                    n = f * NE + e
                    if e + 2 < NE:
                        keep_xe(e + 2)
                    dve.wait_ge(y_prod, n + 1)
                    if n >= 2:
                        dve.wait_ge(scattered[e % 2], 32 * (n // 2))
                    y = yv[:, e % 2, :, :]
                    V.step(tt(y[:, :, 0:D], ps[:, 6 + e % 2, 0:2 * P].rearrange("p (h d) -> p h d", h=2),
                              b2[:, e:e + 1, :].to_broadcast([P, 2, D]), ALU.add))
                    for h in range(2):
                        V.did(ts(y[:, h, 0:D], y[:, h, 0:D], XE[:, e % RX, h, D + e:D + e + 1], None, ALU.mult))
                    nc.vector.tensor_copy(y[:, :, D:AW], XE[:, e % RX, :, D + e:D + e + 1]).then_inc(y_ready, 1)
                for g in range(NG):
                    t = slice(g * TPG, (g + 1) * TPG)
                    dve.wait_ge(acc_in[g], 32 * (f + 1))
                    V.step(tt(tb[:, t, 0:AW], tb[:, t, 0:AW], acc1[:, t, :], ALU.add))
                    gs = tb[:, t, D:AW].rearrange("p t a -> p (t a)")
                    V.step(stt(rinv[:, t], gs, 0.0, gs, ALU.is_equal, ALU.add))
                    V.step(nc.vector.reciprocal(rinv[:, t], rinv[:, t]))
                    for j in range(g * TPG, (g + 1) * TPG):
                        last = stt(xs[:, j, :], tb[:, j, 0:D], rinv[:, j:j + 1], xs[:, j, :], ALU.mult, ALU.add)
                    last.then_inc(x_ready, 1)
                    if f == 0:
                        dve.wait_ge(x_ready, g + 1)
                        stats(g)

            feed(0)
            scales(2, 1.0, EPS)

            V.settle()
            V.step(stt(s_q, s_mean, -1.0, s_r, ALU.mult, ALU.mult))
            nc.vector.tensor_copy(s_d, s_q).then_inc(shift_ready, 1)

            def take_q(n):
                dve.wait_ge(q_exp, n + 1)
                if n >= 2:
                    dve.wait_ge(qs_ready, HD * (n - 1))
                stt(qn[:, n % 2, :], ps[:, 6, :], 0.0, exq, ALU.max, ALU.add).then_inc(q_ready, 1)

            def take_k(n):
                r = n % 2
                dve.wait_ge(k_exp, n + 1)
                stt(kn[:, r, :], ps[:, 5, :], 0.0, exk, ALU.max, ALU.add).then_inc(k_ready, 1)
                dve.wait_ge(k_ready, n + 1)
                if n % NK:
                    dve.wait_ge(z_ready, n)
                nc.vector.tensor_tensor_scan(Zs[:, r, :], kn[:, r, :], kn[:, r, :], Zs[:, 1 - r, GW - 1:GW] if n % NK else 0.0,
                                             ALU.add, ALU.max).then_inc(z_ready, 1)

            def times_k(u):
                dve.wait_ge(v_prod, u + 1)
                if u >= 3:
                    dve.wait_ge(state_ready, u - 2)
                tt(KV[:, u % 3, :], ps[:, u % 4, :], kn[:, u // HD % 2, :], ALU.mult).then_inc(v_used, 1)

            def running_sum(u):
                n, i = divmod(u, HD)
                r = n % 2
                dve.wait_ge(v_used, u + 1)
                if n >= 2:
                    dve.wait_ge(qs_ready, u - 2 * HD + 1)
                if n % NK:
                    dve.wait_ge(state_ready, u - HD + 1)
                nc.vector.tensor_tensor_scan(ST[:, r, i, :], ones[:, 0:1].to_broadcast([P, GW]), KV[:, u % 3, :], ST[:, 1 - r, i, GW - 1:GW] if n % NK else 0.0,
                                             ALU.mult, ALU.add).then_inc(state_ready, 1)

            def take_den(n):
                dve.wait_ge(den_prod, n + 1)
                if n >= 1:
                    dve.wait_ge(rd_ready, n)
                V.step(ts(rden, ps[:, 6, 0:TPG * NH], 1e-6 * HD ** 0.5, None, ALU.max))
                nc.vector.reciprocal(rden, rden).then_inc(rden_ready, 1)

            def divide(n):
                dve.wait_ge(num_prod, 2 * (n + 1))
                dve.wait_ge(rs_ready, n + 1)
                if n >= 2:
                    dve.wait_ge(fin_prod, n - 1)
                tt(On[:, n % 2, :], ps[:, 4, :], RS, ALU.mult).then_inc(on_ready, 1)

            def add_out(n):
                dve.wait_ge(fin_prod, n + 1)
                row = xs[:, n * TPG:(n + 1) * TPG, :].rearrange("p t d -> p (t d)")
                tt(row, row, ps[:, 7, :], ALU.add).then_inc(x3_ready, 1)
                dve.wait_ge(x3_ready, n + 1)
                stats(n)

            take_q(0)
            take_k(0)
            times_k(0)
            for n in range(NG + 2):
                for i in range(HD):
                    u = n * HD + i
                    if i == HD - 1 and n + 1 < NG:
                        dve.wait_ge(k_ready, n + 2)
                    if u + 1 < NG * HD:
                        times_k(u + 1)
                    if n < NG:
                        running_sum(u)
                    if i == 1 and n >= 2:
                        add_out(n - 2)
                    if i == 3 and n + 1 < NG:
                        take_q(n + 1)
                    if i == 4 and n + 1 < NG:
                        take_k(n + 1)
                    if i == 5 and 1 <= n <= NG:
                        divide(n - 1)
                    if i == 7 and n < NG:
                        take_den(n)
            feed(1)


def kernel(**inputs):
    import numpy as np
    import concourse.bacc as bacc
    from concourse.bass_utils import run_bass_kernel_spmd as run

    i = {k[3:]: np.asarray(v) for k, v in inputs.items()}
    inner, dim = i["attn_a_w_out"].shape[1], i["attn_a_w_out"].shape[0]
    E, F, _ = i["ffn_fc1_weight"].shape
    p = 128
    arrays = {
        "x": i["attn_a_x"],
        "wa": i["attn_a_w_a"].reshape(inner, 2, dim).transpose(2, 1, 0),
        "wx": i["attn_a_w_x"].reshape(inner, 2, dim).transpose(2, 1, 0),
        "wo": i["attn_a_w_out"].T,
        "vr": i["attn_a_mat_v_real"], "vi": i["attn_a_mat_v_imag"],
        "vrT": i["attn_a_mat_v_real"].T, "viT": i["attn_a_mat_v_imag"].T,
        "h0r": i["attn_a_last_hidden_real"].reshape(inner, 1), "h0i": i["attn_a_last_hidden_imag"].reshape(inner, 1),
        "wqkvT": i["attn_b_W_qkv"].T, "woutT": i["attn_b_W_out"].T.reshape(dim // 8, 8, dim).transpose(1, 0, 2).reshape(dim, dim),
        "nw": i["ffn_norm_weight"].reshape(dim, 1),
        "rwT": i["ffn_router_weight"].T, "rb": i["ffn_router_bias"].reshape(E, 1),
        "f1T": i["ffn_fc1_weight"].transpose(2, 0, 1),
        "f1b": i["ffn_fc1_bias"].reshape(E, F // p, p).transpose(2, 0, 1),
        "f2T": i["ffn_fc2_weight"].reshape(E, dim, F // p, p).transpose(3, 0, 2, 1),
        "f2b": i["ffn_fc2_bias"],
    }
    arrays = {k: np.ascontiguousarray(v) for k, v in arrays.items()}
    nc = bacc.Bacc("TRN2", target_bir_lowering=False, num_devices=1)
    args = {k: nc.dram_tensor(f"in_{k}", v.shape, mybir.dt.from_np(v.dtype), kind="ExternalInput").ap() for k, v in arrays.items()}
    args["out"] = nc.dram_tensor("out_0", arrays["x"].shape, F32, kind="ExternalOutput").ap()
    build(nc, **args)
    r = run(nc, [{f"in_{k}": v for k, v in arrays.items()}], core_ids=[0])
    return r.results[0]["out_0"]
```
